# Optimizing a Trainium2 kernel written in Bass

```python
import numpy as np
import jax
import jax.numpy as jnp

def _softmax(x, axis=-1):
    return jax.nn.softmax(x, axis=axis)
def _gelu(x):
    return jax.nn.gelu(x, approximate=True)
def _silu(x):
    return jax.nn.silu(x)
def _sigmoid(x):
    return jax.nn.sigmoid(x)
def _layernorm(x, axis=-1, eps=1e-5):
    m = jnp.mean(x, axis=axis, keepdims=True)
    v = jnp.var(x, axis=axis, keepdims=True)
    return (x - m) / jnp.sqrt(v + eps)
def _scatter_add(tgt, idx, src, axis=0):
    return tgt.at[idx].add(src)
def _segment_sum(src, seg, n):
    return jax.ops.segment_sum(src, seg, n)

kernel_name = 'mk_conv_seq_d1_conv_nhwc256_42acf7'

def setup_inputs(seed: int = 0):
    np.random.seed(seed)
    _w = jnp.asarray
    def _rec_inputs():
        import jax
        import jax.numpy as jnp
        _gk = jax.random.key(seed)
        x = -0.0003482 + 1 * jax.random.normal(jax.random.fold_in(_gk, 1), (8, 96, 96, 256), jnp.float32)
        return x
    x = _rec_inputs()
    def _L0_conv_setup():
        import jax, jax.numpy as jnp
        import numpy as np
        D = 256
        K = 3
        A_EPS = 0.0001
        POW_MIN = 1e-20
        LN_EPS = 1e-05

        def _ssm_scan(x, a_logit, b, c, d):
            L = x.shape[1]
            a = jnp.clip(jax.nn.sigmoid(a_logit), A_EPS, 1.0 - A_EPS)
            t = jnp.arange(L, dtype=jnp.float32)
            a_pow = jnp.maximum(jnp.exp(t[:, None] * jnp.log(a)[None, :]), POW_MIN)
            u = x * b
            r = jnp.cumsum(u / a_pow[None], axis=1)
            return r * a_pow[None] * c + x * d
        key = jax.random.key(seed)
        ks = jax.random.split(key, 10)
        B, H, W = (8, 96, 96)
        x = jax.random.normal(ks[0], (B, H, W, D), dtype=jnp.float32)
        inp = {'x': x, 'ln_g': jnp.ones((D,), jnp.float32), 'ln_b': jnp.zeros((D,), jnp.float32), 'w_in': jax.random.normal(ks[1], (D, 2 * D), jnp.float32) * 0.02, 'b_in': jnp.zeros((2 * D,), jnp.float32), 'conv_w': jax.random.normal(ks[2], (K, K, 1, D), jnp.float32) * 0.1, 'conv_b': jnp.zeros((D,), jnp.float32), 'a_logit': 7.0 + 0.1 * jax.random.normal(ks[3], (D,), jnp.float32), 'ssm_b': jnp.ones((D,), jnp.float32) + 0.02 * jax.random.normal(ks[4], (D,), jnp.float32), 'ssm_c': jnp.ones((D,), jnp.float32) + 0.02 * jax.random.normal(ks[5], (D,), jnp.float32), 'ssm_d': jnp.ones((D,), jnp.float32) + 0.02 * jax.random.normal(ks[6], (D,), jnp.float32), 'w_out': jax.random.normal(ks[7], (D, D), jnp.float32) * 0.02, 'b_out': jnp.zeros((D,), jnp.float32)}
        return inp
    _L0_conv_all = _L0_conv_setup()
    _L0_conv_in = {k: v for k, v in _L0_conv_all.items() if k in ('ln_g', 'ln_b', 'w_in', 'b_in', 'conv_w', 'conv_b', 'a_logit', 'ssm_b', 'ssm_c', 'ssm_d', 'w_out', 'b_out', )}
    del _L0_conv_all

    return {
        "x": x,
        "L0_conv_ln_g": _L0_conv_in["ln_g"],
        "L0_conv_ln_b": _L0_conv_in["ln_b"],
        "L0_conv_w_in": _L0_conv_in["w_in"],
        "L0_conv_b_in": _L0_conv_in["b_in"],
        "L0_conv_conv_w": _L0_conv_in["conv_w"],
        "L0_conv_conv_b": _L0_conv_in["conv_b"],
        "L0_conv_a_logit": _L0_conv_in["a_logit"],
        "L0_conv_ssm_b": _L0_conv_in["ssm_b"],
        "L0_conv_ssm_c": _L0_conv_in["ssm_c"],
        "L0_conv_ssm_d": _L0_conv_in["ssm_d"],
        "L0_conv_w_out": _L0_conv_in["w_out"],
        "L0_conv_b_out": _L0_conv_in["b_out"],
    }

def reference(x, L0_conv_ln_g, L0_conv_ln_b, L0_conv_w_in, L0_conv_b_in, L0_conv_conv_w, L0_conv_conv_b, L0_conv_a_logit, L0_conv_ssm_b, L0_conv_ssm_c, L0_conv_ssm_d, L0_conv_w_out, L0_conv_b_out):
    import jax
    import jax.numpy as jnp
    def _L0_conv_ref(x, ln_g, ln_b, w_in, b_in, conv_w, conv_b, a_logit, ssm_b, ssm_c, ssm_d, w_out, b_out):
        import jax, jax.numpy as jnp
        import numpy as np
        D = 256
        K = 3
        A_EPS = 0.0001
        POW_MIN = 1e-20
        LN_EPS = 1e-05

        def _ssm_scan(x, a_logit, b, c, d):
            L = x.shape[1]
            a = jnp.clip(jax.nn.sigmoid(a_logit), A_EPS, 1.0 - A_EPS)
            t = jnp.arange(L, dtype=jnp.float32)
            a_pow = jnp.maximum(jnp.exp(t[:, None] * jnp.log(a)[None, :]), POW_MIN)
            u = x * b
            r = jnp.cumsum(u / a_pow[None], axis=1)
            return r * a_pow[None] * c + x * d
        B, H, W, Dm = x.shape
        x0 = x
        mu = jnp.mean(x, axis=-1, keepdims=True)
        var = jnp.mean(jnp.square(x - mu), axis=-1, keepdims=True)
        h = (x - mu) * jax.lax.rsqrt(var + LN_EPS) * ln_g + ln_b
        xg = h @ w_in + b_in
        x_in, gate = jnp.split(xg, 2, axis=-1)
        gate = jax.nn.sigmoid(gate)
        u = jax.lax.conv_general_dilated(x_in, conv_w, window_strides=(1, 1), padding='SAME', dimension_numbers=('NHWC', 'HWIO', 'NHWC'), feature_group_count=Dm)
        u = jax.nn.silu(u + conv_b)
        L = H * W
        seq_row = u.reshape(B, L, Dm)
        seq_col = u.transpose(0, 2, 1, 3).reshape(B, L, Dm)

        def bid(s):
            yf = _ssm_scan(s, a_logit, ssm_b, ssm_c, ssm_d)
            yb = jnp.flip(_ssm_scan(jnp.flip(s, axis=1), a_logit, ssm_b, ssm_c, ssm_d), axis=1)
            return 0.5 * (yf + yb)
        y_row = bid(seq_row).reshape(B, H, W, Dm)
        y_col = bid(seq_col).reshape(B, W, H, Dm).transpose(0, 2, 1, 3)
        y = 0.5 * (y_row + y_col)
        y = y * gate
        y = y @ w_out + b_out
        return x0 + y

    def _gn(v, G=32, eps=1e-5):
        B_, H_, W_, C_ = v.shape
        g = v.reshape(B_, H_, W_, G, C_ // G)
        m = jnp.mean(g, axis=(1, 2, 4), keepdims=True)
        s = jnp.var(g, axis=(1, 2, 4), keepdims=True)
        return ((g - m) / jnp.sqrt(s + eps)).reshape(v.shape)

    def _ln_c(v, eps=1e-6):
        m = jnp.mean(v, axis=-1, keepdims=True)
        s = jnp.var(v, axis=-1, keepdims=True)
        return (v - m) / jnp.sqrt(s + eps)

    def _ln_t(v, eps=1e-5):
        m = jnp.mean(v, axis=-1, keepdims=True)
        s = jnp.var(v, axis=-1, keepdims=True)
        return (v - m) / jnp.sqrt(s + eps)

    def _to_tokens(v):
        B_, H_, W_, C_ = v.shape
        return v.reshape(B_, H_ * W_, C_)
    def _from_tokens(t, like):
        return t.reshape(like.shape)

    x = _L0_conv_ref(x, L0_conv_ln_g, L0_conv_ln_b, L0_conv_w_in, L0_conv_b_in, L0_conv_conv_w, L0_conv_conv_b, L0_conv_a_logit, L0_conv_ssm_b, L0_conv_ssm_c, L0_conv_ssm_d, L0_conv_w_out, L0_conv_b_out)
    return x


_drawn_inputs = setup_inputs


def setup_inputs(seed=0):
    import zlib

    import numpy as np

    out = dict(_drawn_inputs(seed))
    spreads = {'L0_conv_ln_g': (1.0, 0.2),
     'L0_conv_ln_b': (0.0, 0.1),
     'L0_conv_b_in': (0.0, 0.1),
     'L0_conv_conv_b': (0.0, 0.1),
     'L0_conv_b_out': (0.0, 0.1)}
    factors = {}
    for name, (base, spread) in spreads.items():
        noise = np.random.default_rng([zlib.crc32(name.encode()), seed]).standard_normal(out[name].shape)
        drawn = base * np.exp(spread * noise) if base else spread * noise
        out[name] = jnp.asarray(drawn.astype(out[name].dtype))
    for name, factor in factors.items():
        out[name] = (out[name] * factor).astype(out[name].dtype)
    return out
```

```python
import math
from contextlib import ExitStack

import concourse.bass as bass
from concourse import mybir

F32 = mybir.dt.float32
BF16 = mybir.dt.bfloat16
ALU = mybir.AluOpType
ACT = mybir.ActivationFunctionType

P = 128
A_EPS = 1e-4
POW_MIN = 1e-20
LN_EPS = 1e-5
TINY = 1e-18
QUARTERS = 4
STEPS = 3

PE_TAPS = [(0, 0), (-1, -1), (-1, 1), (1, -1), (1, 1)]
DVE_TAPS = [(-1, 0), (1, 0), (0, -1), (0, 1)]


def finished(g):
    return g + 2


def before(g):
    return g + 1


def run_periods(eng, period, images):
    last = 2 * images - 1
    for n in (-3, -2):
        period(n, n % 2, x=True)
    period(-1, 1, x=True, conv=True)
    for n in (0, 1):
        period(n, n % 2, x=True, conv=True, scan=True)
    with eng.Fori(1, images - 2) as pair:
        period(2 * pair, 0, x=True, conv=True, scan=True, gate=True)
        period(2 * pair + 1, 1, x=True, conv=True, scan=True, gate=True)
    period(last - 3, 0, x=True, conv=True, scan=True, gate=True)
    for n in (last - 2, last - 1):
        period(n, n % 2, conv=True, scan=True, gate=True)
    period(last, 1, scan=True, gate=True)
    for n in (last + 1, last + 2):
        period(n, n % 2, gate=True)


def conv_seq_kernel(nc, x, ln_g, ln_b, w_in, b_in, conv_w, conv_b, a_logit, ssm_b, ssm_c, ssm_d,
                    w_out, b_out, ident_in, steps_in, out):
    IMAGES, HH, WW, D = x.shape
    L = HH * WW
    KH = D // P
    JOB = 3 * P
    TILES = JOB // P
    PER_UNIT = QUARTERS * STEPS
    CH = L // PER_UNIT
    CR = CH // WW
    HALF = PER_UNIT // 2
    QR = HH // QUARTERS
    ROWS = HH + 3
    UNITS = KH * IMAGES
    JOBS = IMAGES * L // JOB
    NT = len(PE_TAPS)
    ND = len(DVE_TAPS)
    LOG_MIN = math.log(POW_MIN)
    assert KH == 2 and L % JOB == 0 and CH == 2 * JOB and CR * WW == CH and JOB == 4 * WW

    x_t = x.rearrange("b h w d -> (b h w) d").rearrange("(g i p) d -> g p i d", i=TILES, p=P)
    out_t = out.rearrange("b h w d -> (b h w) d").rearrange("(g i p) d -> g p i d", i=TILES, p=P)
    xin_d = nc.dram_tensor("xin_scratch", [IMAGES, KH, P, L], F32, kind="Internal").ap()
    s_d = nc.dram_tensor("scan_scratch", [IMAGES, KH, P, L], F32, kind="Internal").ap()
    tab_d = nc.dram_tensor("ratio_scratch", [KH, P, L], F32, kind="Internal").ap()

    ctx = ExitStack()
    with ctx:
        def sb(name, shape, dt=F32):
            return ctx.enter_context(nc.sbuf_tensor(name, shape, dt))

        def ps(name, shape):
            return ctx.enter_context(nc.psum_tensor(name, shape, F32))

        def sem(name):
            return ctx.enter_context(nc.semaphore(name))

        slot = [sb(f"slot{j}", [P, ROWS, WW]) for j in range(KH)]
        slotf = [s[:, :, :].rearrange("p h w -> p (h w)") for s in slot]
        u_col = sb("u_col", [P, WW, HH])
        ucf = u_col[:, :, :].rearrange("p w h -> p (w h)")
        hs = sb("hs", [P, L])
        tab = sb("tab", [P, 2, CH])
        state = sb("state", [P, 2])
        xa = sb("xa", [P, TILES, D])
        xn_x = sb("xn_x", [P, TILES, D])
        xt_x = sb("xt_x", [P, KH, JOB])
        xs = sb("xs", [P, KH, JOB])
        bst = sb("bst", [P, TILES, 6])
        pre = sb("pre", [P, CR, WW])
        xg = sb("xg", [P, TILES, D])
        xn_g = sb("xn_g", [P, TILES, D])
        xt_g = sb("xt_g", [P, KH, JOB])
        y = sb("y", [P, KH, JOB])
        sg = sb("sg", [P, KH, JOB])
        ln_all = sb("ln_all", [P, JOBS, 2 * TILES])
        ln_x = sb("ln_x", [P, 2 * TILES])
        ln_gt = sb("ln_gt", [P, 2 * TILES])
        lt = sb("lt", [P, 4, TILES])
        mhalf = sb("mhalf", [P, TILES])
        w_in_sb = sb("w_in_sb", [P, KH, 2 * D])
        w_out_sb = sb("w_out_sb", [P, KH, D])
        ident = sb("ident", [P, P])
        diag = sb("diag", [P, NT, KH, P])
        cw = sb("cw", [P, 9, KH])
        cols = sb("cols", [P, 10, KH])
        g_c, b_c, bx_c, bg_c, cb_c, al_c, sb_c, sc_c, sd_c, kap = [cols[:, i, :] for i in range(10)]
        more = sb("more", [P, 6, KH])
        a_c, la_c, nla_c, del_c, hbg_c, tmp_c = [more[:, i, :] for i in range(6)]
        bo = sb("bo", [P, D])
        bo_rest = sb("bo_rest", [P, D])
        bo_part = sb("bo_part", [P, D], BF16)
        bo3 = sb("bo3", [P, D], BF16)
        ones3 = sb("ones3", [P, P], BF16)

        ps_x = ps("ps_x", [P, 2, 512])
        ps_g = ps("ps_g", [P, 2, 512])
        ps_c = ps("ps_c", [P, 2, 512])
        ps_o = ps("ps_o", [P, 2, 512])
        ps_of = ps_o[:, :, :].rearrange("p a b -> p (a b)")

        set_in = sem("set_in")
        set_steps = sem("set_steps")
        set_v = sem("set_v")
        set_a = sem("set_a")
        set_done = sem("set_done")
        tab_made = sem("tab_made")
        passed = sem("passed")
        tab_stored = sem("tab_stored")
        x_loaded = sem("x_loaded")
        x_stats = sem("x_stats")
        x_norm = sem("x_norm")
        x_turned = sem("x_turned")
        x_evac = sem("x_evac")
        x_proj = sem("x_proj")
        x_out = sem("x_out")
        xin_stored = sem("xin_stored")
        ln_step = sem("ln_step")
        ln_copied = sem("ln_copied")
        xin_loaded = [sem(f"xin_loaded{q}") for q in range(QUARTERS)]
        halo_zero = sem("halo_zero")
        conv_summed = sem("conv_summed")
        conv_tap = sem("conv_tap")
        silu_done = sem("silu_done")
        conv_out = sem("conv_out")
        tab_loaded = [sem(f"tab_loaded{k}") for k in range(2)]
        scan_f = sem("scan_f")
        scan_b = sem("scan_b")
        ucol_ready = sem("ucol_ready")
        state_saved = sem("state_saved")
        d_added = sem("d_added")
        rows_done = sem("rows_done")
        cols_done = sem("cols_done")
        s_ready = sem("s_ready")
        s_stored = [sem(f"s_stored{q}") for q in range(QUARTERS)]
        xg_loaded = sem("xg_loaded")
        sg_loaded = sem("sg_loaded")
        g_norm = sem("g_norm")
        g_turned = sem("g_turned")
        g_evac = sem("g_evac")
        g_proj = sem("g_proj")
        g_act = sem("g_act")
        y_done = sem("y_done")
        o_proj = sem("o_proj")
        o_added = sem("o_added")
        o_stored = sem("o_stored")

        N_IN = 15

        def base(eng, *sems, by=1):
            for s in sems:
                eng.sem_inc(s, by)

        def wait_alone(eng, s, value):
            eng.wait_ge(s, value)
            eng.sem_inc(passed, 1)

        def x_job(n, s):
            return (n + 3) * PER_UNIT + s

        def g_job(n, s):
            return (n - 2) * PER_UNIT + s

        def tap_done(g, t):
            return g * ND + t + 2

        block = ctx.enter_context(nc.Block())

        @block.sync
        def _(sp):
            def col(v, width=KH):
                return v.rearrange("(j p) -> p j", p=P)

            with nc.allow_non_contiguous_dma(reason="small per-channel vectors, once"):
                sp.dma_start(w_in_sb[:, :, :], w_in.rearrange("(k p) n -> p k n", p=P)).then_inc(set_in, 16)
                sp.dma_start(w_out_sb[:, :, :], w_out.rearrange("(k p) n -> p k n", p=P)).then_inc(set_in, 16)
                sp.dma_start(ident[:, :], ident_in).then_inc(set_in, 16)
                for dst, src in ((g_c, col(ln_g)), (b_c, col(ln_b)), (cb_c, col(conv_b)), (al_c, col(a_logit)),
                                 (sb_c, col(ssm_b)), (sc_c, col(ssm_c)), (sd_c, col(ssm_d)),
                                 (bx_c, col(b_in[0:D])), (bg_c, col(b_in[D:2 * D]))):
                    sp.dma_start(dst, src).then_inc(set_in, 16)
                cwv = conv_w.rearrange("a b o (j p) -> p (a b o) j", p=P)
                for j in range(KH):
                    sp.dma_start(cw[:, :, j], cwv[:, :, j]).then_inc(set_in, 16)
                sp.dma_start(bo[:, :], b_out.rearrange("(o d) -> o d", o=1).broadcast_to([P, D])).then_inc(set_in, 16)
                sp.dma_start(ucf, steps_in.broadcast_to([P, L])).then_inc(set_steps, 16)
            base(sp, xin_stored, o_stored, by=16)
            for j in range(KH):
                sp.wait_ge(tab_made, j + 1)
                sp.dma_start(tab_d[j], hs[:, :]).then_inc(tab_stored, 16)
                sp.wait_ge(tab_stored, 16 * (j + 1))

            def period(n, par, x=False, conv=False, scan=False, gate=False):
                for q in range(QUARTERS):
                    if conv and q == 0:
                        img = (n + 1) // 2 if isinstance(n, int) else None
                        if img is None:
                            m_img = xin_image(n, par)
                        else:
                            m_img = img
                        wait_alone(sp, xin_stored, (m_img + 1) * (16 * L // JOB) + 16)
                        j = (par + 1) % 2
                        for r in range(QUARTERS):
                            if not isinstance(n, int) or n >= 1:
                                wait_alone(sp, s_stored[min(r + 1, 3)], 16 * n)
                                sp.wait_ge(s_stored[r], 16 * n)
                            sp.dma_start(slot[j][:, 2 + QR * r:2 + QR * (r + 1), :].rearrange("p h w -> p (h w)"),
                                         xin_d[m_img, j, :, QR * WW * r:QR * WW * (r + 1)]
                                         ).then_inc(xin_loaded[r], 16)
                    if gate and q == 0 and par == 0:
                        for r in range(QUARTERS):
                            wait_alone(sp, s_stored[r], 16 * n)
                    with sp.Fori(0, STEPS) as i:
                        s = i + q * STEPS
                        if scan:
                            for k in range(2):
                                pr = n * (2 * PER_UNIT) + (2 * s + k)
                                wait_alone(sp, scan_b, pr + 1)
                                c = (i * 2 + (HALF * (q % 2) + k))
                                sp.dma_start(tab[:, k, :], tab_d[par, :, bass.ds(c * CH, CH)]
                                             ).then_inc(tab_loaded[k], 16)
                        if x:
                            g = x_job(n, s)
                            wait_alone(sp, x_norm, before(g))
                            sp.dma_start(xa[:, :, :], x_t[bass.ds(g, 1)].rearrange("o p i d -> (o p) i d")
                                         ).then_inc(x_loaded, 16)
                        if gate:
                            g = g_job(n, s)
                            img = g_image(n, par)
                            wait_alone(sp, o_stored, g * 16 + 16)
                            sp.dma_start(xg[:, :, :], x_t[bass.ds(g, 1)].rearrange("o p i d -> (o p) i d")
                                         ).then_inc(xg_loaded, 16)
                            wait_alone(sp, y_done, before(g))
                            sp.dma_start(sg[:, :, :],
                                         s_d[img][:, :, bass.ds((s + par * PER_UNIT) * JOB, JOB)]
                                         .rearrange("k p t -> p k t")).then_inc(sg_loaded, 16)
                        if x:
                            g = x_job(n, s)
                            img = x_image(n, par)
                            sl = s + ((par + 1) % 2) * PER_UNIT
                            wait_alone(sp, x_out, finished(g))
                            sp.dma_start(xin_d[img][:, :, bass.ds(sl * JOB, JOB)].rearrange("k p t -> p k t"),
                                         xs[:, :, :]).then_inc(xin_stored, 16)
                        if gate:
                            g = g_job(n, s)
                            wait_alone(sp, o_added, finished(g))
                            sp.dma_start(out_t[bass.ds(g, 1)].rearrange("o p i d -> (o p) i d"), xg[:, :, :]
                                         ).then_inc(o_stored, 16)
                if scan:
                    for r in range(QUARTERS):
                        wait_alone(sp, s_ready, n * QUARTERS + (r + 1))
                        sp.dma_start(s_d[unit_image(n, par), par, :, QR * WW * r:QR * WW * (r + 1)],
                                     slotf[par][:, QR * WW * r:QR * WW * (r + 1)]).then_inc(s_stored[r], 16)

            def half_of(n, par):
                return (n - par) // 2

            def unit_image(n, par):
                return half_of(n, par)

            def xin_image(n, par):
                return half_of(n, par) + par

            def x_image(n, par):
                return half_of(n, par) + 1 + par

            def g_image(n, par):
                return half_of(n, par) - 1

            run_periods(sp, period, IMAGES)
            for r in range(QUARTERS):
                wait_alone(sp, s_stored[r], 16 * UNITS)
            sp.wait_ge(xin_stored, 16 * (JOBS + 1))
            sp.wait_ge(o_stored, 16 * (JOBS + 1))

        @block.tensor
        def _(pe):
            base(pe, x_turned, x_proj, g_turned, g_proj, o_proj, conv_summed)
            pe.wait_ge(set_done, 1)

            def turn(ps_t, src, done):
                for t in range(TILES):
                    for k in range(KH):
                        ins = pe.transpose(ps_t[:, k, t * P:(t + 1) * P], src[:, t, k * P:(k + 1) * P], ident[:, :])
                ins.then_inc(done, 1)

            def project(ps_t, src, first, done):
                for j in range(KH):
                    for k in range(KH):
                        ins = pe.matmul(ps_t[:, j, 0:JOB], w_in_sb[:, k, first + j * P:first + (j + 1) * P],
                                        src[:, k, :], start=(k == 0), stop=(k == KH - 1))
                ins.then_inc(done, 1)

            def conv_taps(j, row, g):
                pe.wait_ge(conv_tap, g * ND + 1)
                for r in range(2):
                    half_rows = CR // 2
                    acc = ps_c[:, r, 0:JOB].rearrange("p (h w) -> p h w", w=WW)
                    for t, (dh, dw) in enumerate(PE_TAPS):
                        lo, hi = max(0, -dw), WW - max(0, dw)
                        ins = pe.matmul(acc[:, :, lo:hi], diag[:, t, j, :],
                                        slot[j][:, bass.ds(row + (half_rows * r + 2 + dh), half_rows), lo + dw:hi + dw],
                                        start=(t == 0), stop=(t == NT - 1))
                ins.then_inc(conv_summed, 1)

            def period(n, par, x=False, conv=False, scan=False, gate=False):
                jc = (par + 1) % 2
                for q in range(QUARTERS):
                    if conv:
                        for r in range(q, min(q + 2, QUARTERS)):
                            wait_alone(pe, xin_loaded[r], ((n + 1)) * 16 + 16)
                        if q == 0:
                            wait_alone(pe, halo_zero, (n + 1) + 1)
                    with pe.Fori(0, STEPS) as i:
                        s = i + q * STEPS
                        if conv:
                            conv_taps(jc, s * CR, (n + 1) * PER_UNIT + s)
                        if gate:
                            g = g_job(n, s)
                            pe.wait_ge(g_norm, finished(g))
                            pe.wait_ge(g_act, before(g))
                            turn(ps_g, xn_g, g_turned)
                        if x:
                            g = x_job(n, s)
                            pe.wait_ge(x_norm, finished(g))
                            pe.wait_ge(x_out, before(g))
                            turn(ps_x, xn_x, x_turned)
                        if gate:
                            g = g_job(n, s)
                            pe.wait_ge(g_evac, finished(g))
                            project(ps_g, xt_g, D, g_proj)
                        if x:
                            g = x_job(n, s)
                            pe.wait_ge(x_evac, finished(g))
                            project(ps_x, xt_x, 0, x_proj)
                        if gate:
                            g = g_job(n, s)
                            pe.wait_ge(y_done, finished(g))
                            pe.wait_ge(o_added, before(g))
                            for t in range(TILES):
                                o = ps_of[:, t * D:(t + 1) * D]
                                pe.matmul(o, ones3[:, :], bo3[:, :], start=True, stop=False)
                                for k in range(KH):
                                    ins = pe.matmul(o, y[:, k, t * P:(t + 1) * P], w_out_sb[:, k, :],
                                                    start=False, stop=(k == KH - 1))
                            ins.then_inc(o_proj, 1)

            run_periods(pe, period, IMAGES)

        @block.scalar
        def _(act):
            base(act, x_evac, x_out, g_evac, g_act, conv_out, silu_done)
            act.wait_ge(set_in, 16 * N_IN)
            act.activation(tmp_c, al_c, ACT.Exp, scale=-1.0).then_inc(set_a, 1)
            act.wait_ge(set_v, 3)
            act.activation(la_c, a_c, ACT.Ln).then_inc(set_a, 1)
            for j in range(KH):
                act.wait_ge(set_v, 6 + 2 * j)
                act.activation(hs[:, :], hs[:, :], ACT.Exp).then_inc(set_a, 1)
            act.wait_ge(set_done, 1)

            def period(n, par, x=False, conv=False, scan=False, gate=False):
                jc = (par + 1) % 2
                for q in range(QUARTERS):
                    if scan and q == 0:
                        act.wait_ge(conv_out, finished(n * PER_UNIT + (PER_UNIT - 1)))
                        if not isinstance(n, int) or n >= 1:
                            act.wait_ge(s_ready, QUARTERS * n)
                    with act.Fori(0, STEPS) as i:
                        s = i + q * STEPS
                        if gate:
                            g = g_job(n, s)
                            act.wait_ge(g_turned, finished(g))
                            act.wait_ge(g_proj, before(g))
                            for k in range(KH):
                                ins = act.activation(xt_g[:, k, :], ps_g[:, k, 0:JOB], ACT.Identity,
                                                     bias=b_c[:, k:k + 1], scale=g_c[:, k:k + 1])
                            ins.then_inc(g_evac, 1)
                        if x:
                            g = x_job(n, s)
                            act.wait_ge(x_turned, finished(g))
                            act.wait_ge(x_proj, before(g))
                            for k in range(KH):
                                ins = act.activation(xt_x[:, k, :], ps_x[:, k, 0:JOB], ACT.Identity,
                                                     bias=b_c[:, k:k + 1], scale=g_c[:, k:k + 1])
                            ins.then_inc(x_evac, 1)
                        if scan and q == 0:
                            R = HH // STEPS
                            ins = act.activation(u_col[:, :, bass.ds(i * R, R)].rearrange("p w h -> p h w"),
                                                 slot[par][:, bass.ds(i * R, R), :], ACT.Copy)
                            ins.then_inc(ucol_ready, 1)
                        if gate:
                            g = g_job(n, s)
                            act.wait_ge(g_proj, finished(g))
                            act.wait_ge(o_proj, before(g))
                            for j in range(KH):
                                ins = act.activation(y[:, j, :], ps_g[:, j, 0:JOB], ACT.Tanh,
                                                     bias=hbg_c[:, j:j + 1], scale=0.5)
                            ins.then_inc(g_act, 1)
                        if x:
                            g = x_job(n, s)
                            act.wait_ge(x_proj, finished(g))
                            act.wait_ge(xin_stored, g * 16 + 16)
                            for j in range(KH):
                                ins = act.activation(xs[:, j, :], ps_x[:, j, 0:JOB], ACT.Identity,
                                                     bias=bx_c[:, j:j + 1])
                            ins.then_inc(x_out, 1)
                        if conv:
                            g = (n + 1) * PER_UNIT + s
                            act.wait_ge(conv_tap, tap_done(g, ND - 1))
                            act.activation(pre[:, :, :], pre[:, :, :], ACT.Silu,
                                           bias=cb_c[:, jc:jc + 1]).then_inc(silu_done, 1)
                            act.wait_ge(silu_done, finished(g))
                            act.activation(slot[jc][:, bass.ds(s * CR, CR), :], pre[:, :, :], ACT.Copy,
                                           scale=kap[:, jc:jc + 1]).then_inc(conv_out, 1)

            run_periods(act, period, IMAGES)

        @block.gpsimd
        def _(pool):
            base(pool, x_norm, g_norm, ln_step)
            pool.memset(mhalf[:, :], -0.5).then_inc(ln_step, 1)
            LN_OPS = 10

            def period(n, par, x=False, conv=False, scan=False, gate=False):
                jc = (par + 1) % 2
                if conv:
                    if not isinstance(n, int) or n >= 1:
                        wait_alone(pool, s_stored[0], 16 * n)
                    pool.memset(slot[jc][:, 1, :], 0.0).then_inc(halo_zero, 1)
                for q in range(QUARTERS):
                    with pool.Fori(0, STEPS) as i:
                        s = i + q * STEPS
                        if x:
                            g = x_job(n, s)
                            c = g * LN_OPS + 2
                            pool.wait_ge(x_stats, finished(g))
                            pool.wait_ge(ln_step, c)
                            pool.tensor_tensor(lt[:, 0, :], bst[:, :, 1], bst[:, :, 4], ALU.add).then_inc(ln_step, 1)
                            pool.tensor_tensor(lt[:, 1, :], bst[:, :, 1], bst[:, :, 4], ALU.subtract).then_inc(ln_step, 1)
                            pool.tensor_tensor(lt[:, 2, :], bst[:, :, 2], bst[:, :, 5], ALU.add).then_inc(ln_step, 1)
                            pool.wait_ge(ln_step, c + 3)
                            pool.tensor_tensor(lt[:, 1, :], lt[:, 1, :], lt[:, 1, :], ALU.mult).then_inc(ln_step, 1)
                            wait_alone(pool, ln_step, c + 4)
                            pool.tensor_scalar(lt[:, 1, :], lt[:, 1, :], D / 4.0, 0.0, ALU.mult, ALU.add).then_inc(ln_step, 1)
                            pool.wait_ge(ln_step, c + 5)
                            pool.tensor_tensor(lt[:, 2, :], lt[:, 1, :], lt[:, 2, :], ALU.add).then_inc(ln_step, 1)
                            wait_alone(pool, ln_step, c + 6)
                            pool.tensor_scalar(lt[:, 2, :], lt[:, 2, :], 1.0 / D, LN_EPS, ALU.mult, ALU.add).then_inc(ln_step, 1)
                            pool.wait_ge(ln_step, c + 7)
                            pool.tensor_tensor(ln_x[:, 0:TILES], lt[:, 2, :], mhalf[:, :], ALU.pow).then_inc(ln_step, 1)
                            pool.tensor_scalar(lt[:, 0, :], lt[:, 0, :], -0.5, 0.0, ALU.mult, ALU.add).then_inc(ln_step, 1)
                            pool.wait_ge(ln_step, c + 9)
                            pool.tensor_tensor(ln_x[:, TILES:2 * TILES], lt[:, 0, :], ln_x[:, 0:TILES], ALU.mult).then_inc(ln_step, 1)
                            pool.wait_ge(ln_step, c + 10)
                            pool.tensor_copy(ln_all[:, bass.ds(g, 1), :].rearrange("p o t -> p (o t)"), ln_x[:, :])
                            wait_alone(pool, x_turned, before(g))
                            for t in range(TILES):
                                ins = pool.tensor_scalar(xn_x[:, t, :], xa[:, t, :], ln_x[:, t:t + 1],
                                                         ln_x[:, TILES + t:TILES + t + 1], ALU.mult, ALU.add)
                            ins.then_inc(x_norm, 1)
                        if gate:
                            g = g_job(n, s)
                            pool.wait_ge(g_norm, before(g))
                            pool.tensor_copy(ln_gt[:, :], ln_all[:, bass.ds(g, 1), :].rearrange("p o t -> p (o t)")
                                             ).then_inc(ln_copied, 1)
                            pool.wait_ge(ln_copied, g + 1)
                            pool.wait_ge(xg_loaded, g * 16 + 16)
                            wait_alone(pool, g_turned, before(g))
                            for t in range(TILES):
                                ins = pool.tensor_scalar(xn_g[:, t, :], xg[:, t, :], ln_gt[:, t:t + 1],
                                                         ln_gt[:, TILES + t:TILES + t + 1], ALU.mult, ALU.add)
                            ins.then_inc(g_norm, 1)

            run_periods(pool, period, IMAGES)

        @block.vector
        def _(dve):
            base(dve, x_stats, conv_tap, scan_f, y_done, o_added)
            base(dve, scan_b, by=2)
            for j in range(KH):
                dve.memset(slot[j][:, ROWS - 1, :], 0.0)
            dve.memset(ones3[:, :], 1.0)

            dve.wait_ge(set_a, 1)
            dve.tensor_scalar(tmp_c, tmp_c, 1.0, None, ALU.add).then_inc(set_v, 1)
            dve.wait_ge(set_v, 1)
            dve.reciprocal(tmp_c, tmp_c).then_inc(set_v, 1)
            dve.wait_ge(set_v, 2)
            dve.tensor_scalar(a_c, tmp_c, A_EPS, 1.0 - A_EPS, ALU.max, ALU.min).then_inc(set_v, 1)
            dve.wait_ge(set_a, 2)
            dve.tensor_scalar(nla_c, la_c, -1.0, None, ALU.mult).then_inc(set_v, 1)
            dve.wait_ge(set_v, 4)
            dve.wait_ge(set_steps, 16)
            for j in range(KH):
                if j:
                    dve.wait_ge(tab_stored, 16 * j)
                dve.tensor_scalar(hs[:, :], ucf, nla_c[:, j:j + 1], LOG_MIN, ALU.mult, ALU.add).then_inc(set_v, 1)
                dve.wait_ge(set_v, 5 + 2 * j)
                dve.tensor_scalar(hs[:, :], hs[:, :], 0.0, None, ALU.min).then_inc(set_v, 1)
                dve.wait_ge(set_a, 3 + j)
                dve.tensor_scalar(hs[:, :], hs[:, :], 1.0, a_c[:, j:j + 1], ALU.min, ALU.max).then_inc(tab_made, 1)

            dve.wait_ge(set_in, 16 * N_IN)
            dve.tensor_tensor(tmp_c, sb_c, sc_c, ALU.mult).then_inc(set_v, 1)
            dve.wait_ge(set_v, 9)
            dve.tensor_scalar(kap, tmp_c, 0.125, None, ALU.mult).then_inc(set_v, 1)
            dve.wait_ge(set_v, 10)
            dve.tensor_tensor(tmp_c, kap, kap, ALU.mult).then_inc(set_v, 1)
            dve.wait_ge(set_v, 11)
            dve.tensor_scalar(tmp_c, tmp_c, TINY * TINY, 2.0 * TINY, ALU.is_lt, ALU.mult).then_inc(set_v, 1)
            dve.wait_ge(set_v, 12)
            dve.tensor_tensor(kap, kap, tmp_c, ALU.add).then_inc(set_v, 1)
            dve.wait_ge(set_v, 13)
            dve.reciprocal(tmp_c, kap).then_inc(set_v, 1)
            dve.wait_ge(set_v, 14)
            dve.scalar_tensor_tensor(out=del_c, in0=sd_c, scalar=0.5, in1=tmp_c, op0=ALU.mult, op1=ALU.mult
                                     ).then_inc(set_v, 1)
            dve.tensor_scalar(hbg_c, bg_c, 0.5, None, ALU.mult).then_inc(set_v, 1)
            for t, (dh, dw) in enumerate(PE_TAPS):
                tap = (dh + 1) * 3 + dw + 1
                for j in range(KH):
                    dve.tensor_scalar(diag[:, t, j, :], ident[:, :], cw[:, tap, j:j + 1], None, ALU.mult)
            dve.tensor_copy(bo_part[:, :], bo[:, :]).then_inc(set_v, 1)
            dve.wait_ge(set_v, 17)
            dve.tensor_tensor(bo_rest[:, :], bo[:, :], bo_part[:, :], ALU.subtract).then_inc(set_v, 1)
            dve.tensor_scalar(bo3[:, :], bo_part[:, :], ident[:, 0:1], None, ALU.mult).then_inc(set_v, 1)
            for r in range(1, 3):
                dve.wait_ge(set_v, 19 + 3 * (r - 1))
                dve.tensor_copy(bo_part[:, :], bo_rest[:, :]).then_inc(set_v, 1)
                dve.wait_ge(set_v, 20 + 3 * (r - 1))
                dve.tensor_tensor(bo_rest[:, :], bo_rest[:, :], bo_part[:, :], ALU.subtract).then_inc(set_v, 1)
                dve.scalar_tensor_tensor(out=bo3[:, :], in0=bo_part[:, :], scalar=ident[:, r:r + 1], in1=bo3[:, :],
                                         op0=ALU.mult, op1=ALU.add).then_inc(set_v, 1)
            dve.wait_ge(set_v, 25)
            dve.memset(state[:, :], 0.0).then_inc(set_done, 1)

            def tap(j, s, g, t):
                dh, dw = DVE_TAPS[t]
                w = cw[:, (dh + 1) * 3 + dw + 1, j:j + 1]
                row = s * CR + (2 + dh)
                if t == 0:
                    dve.wait_ge(conv_summed, finished(g))
                    dve.wait_ge(conv_out, before(g))
                    dve.scalar_tensor_tensor(
                        out=pre[:, :, :].rearrange("p (a h) w -> p a (h w)", a=2),
                        in0=slot[j][:, bass.ds(row, CR), :].rearrange("p (a h) w -> p a (h w)", a=2), scalar=w,
                        in1=ps_c[:, :, 0:JOB], op0=ALU.mult, op1=ALU.add).then_inc(conv_tap, 1)
                else:
                    lo, hi = max(0, -dw), WW - max(0, dw)
                    dve.wait_ge(conv_tap, tap_done(g, t - 1))
                    dve.scalar_tensor_tensor(
                        out=pre[:, :, lo:hi], in0=slot[j][:, bass.ds(row, CR), lo + dw:hi + dw], scalar=w,
                        in1=pre[:, :, lo:hi], op0=ALU.mult, op1=ALU.add).then_inc(conv_tap, 1)

            def forward(n, src, phase, c):
                pr = n * (2 * PER_UNIT) + (PER_UNIT * phase + c)
                lo = c * CH
                dve.wait_ge(tab_loaded[c % 2], (n * PER_UNIT + (HALF * phase + c // 2)) * 16 + 16)
                dve.wait_ge(scan_f, before(pr))
                if c == 0:
                    init = 0.0
                elif c < HALF:
                    init = hs[:, lo - 1:lo]
                elif c == HALF:
                    init = state[:, 0:1]
                else:
                    init = src[:, lo - 1:lo]
                dst = hs[:, lo:lo + CH] if c < HALF else src[:, lo:lo + CH]
                dve.tensor_tensor_scan(dst, tab[:, c % 2, :], src[:, lo:lo + CH], init, ALU.mult, ALU.add
                                       ).then_inc(scan_f, 1)

            def backward(n, src, phase, c):
                pr = n * (2 * PER_UNIT) + (PER_UNIT * phase + c)
                lo = L - (c + 1) * CH
                hi = lo + CH
                dve.wait_ge(scan_b, pr + 2)
                if c == 0:
                    init = 0.0
                elif c < HALF:
                    init = hs[:, hi:hi + 1]
                elif c == HALF:
                    init = state[:, 1:2]
                else:
                    init = src[:, hi:hi + 1]
                flip = slice(hi - 1, lo - 1 if lo else None, -1)
                dst = hs[:, flip] if c < HALF else src[:, flip]
                dve.tensor_tensor_scan(dst, tab[:, c % 2, :], src[:, flip], init, ALU.mult, ALU.add
                                       ).then_inc(scan_b, 1)

            def period(n, par, x=False, conv=False, scan=False, gate=False):
                jc = (par + 1) % 2
                u = slotf[par]
                if conv:
                    dve.wait_ge(halo_zero, n + 2)
                    for r in range(QUARTERS):
                        dve.wait_ge(xin_loaded[r], ((n + 1)) * 16 + 16)
                if scan:
                    dve.wait_ge(conv_out, finished(n * PER_UNIT + (PER_UNIT - 1)))

                def step(q, i):
                    s = i + q * STEPS
                    phase, c = q // 2, HALF * (q % 2) + 2 * i
                    src = u if phase == 0 else ucf[:, 0:L]
                    gc = (n + 1) * PER_UNIT + s
                    if x:
                        g = x_job(n, s)
                        dve.wait_ge(x_loaded, g * 16 + 16)
                        for t in range(TILES):
                            ins = dve.bn_stats(bst[:, t, :], xa[:, t, :])
                        ins.then_inc(x_stats, 1)
                    if scan:
                        forward(n, src, phase, c)
                    if conv:
                        tap(jc, s, gc, 0)
                    if scan:
                        backward(n, src, phase, c)
                    if gate:
                        g = g_job(n, s)
                        dve.wait_ge(g_act, finished(g))
                        dve.wait_ge(sg_loaded, g * 16 + 16)
                        dve.scalar_tensor_tensor(out=y[:, :, :], in0=y[:, :, :], scalar=1.0, in1=sg[:, :, :],
                                                 op0=ALU.add, op1=ALU.mult).then_inc(y_done, 1)
                    if conv:
                        tap(jc, s, gc, 1)
                    if scan:
                        forward(n, src, phase, c + 1)
                    if conv:
                        for t in range(2, ND - 1):
                            tap(jc, s, gc, t)
                    if scan:
                        backward(n, src, phase, c + 1)
                    if conv and ND > 2:
                        tap(jc, s, gc, ND - 1)
                    if gate:
                        g = g_job(n, s)
                        dve.wait_ge(o_proj, finished(g))
                        dve.tensor_tensor(xg[:, :, :].rearrange("p t d -> p (t d)"), ps_of[:, 0:TILES * D],
                                          xg[:, :, :].rearrange("p t d -> p (t d)"), ALU.add).then_inc(o_added, 1)

                for q in range(QUARTERS):
                    if not scan:
                        with dve.Fori(0, STEPS) as i:
                            step(q, i)
                        continue
                    if q == 1:
                        dve.wait_ge(ucol_ready, (n + 1) * STEPS)
                    if q == 2:
                        dve.wait_ge(rows_done, n + 1)
                    for i in range(STEPS):
                        step(q, i)
                    pairs = n * (2 * PER_UNIT) + HALF * (q + 1)
                    dve.wait_ge(scan_f, pairs + 1)
                    dve.wait_ge(scan_b, pairs + 2)
                    if q in (0, 2):
                        ph = n * 4 + q
                        dve.tensor_copy(state[:, 0:1], hs[:, L // 2 - 1:L // 2]).then_inc(state_saved, 1)
                        dve.tensor_copy(state[:, 1:2], hs[:, L // 2:L // 2 + 1]).then_inc(state_saved, 1)
                        dve.wait_ge(state_saved, ph + 2)
                    if q == 0:
                        dve.scalar_tensor_tensor(out=hs[:, :], in0=u[:, 0:L], scalar=del_c[:, par:par + 1],
                                                 in1=hs[:, :], op0=ALU.mult, op1=ALU.add).then_inc(d_added, 1)
                        dve.wait_ge(d_added, n + 1)
                    if q == 1:
                        dve.tensor_tensor(u[:, 0:L], u[:, 0:L], hs[:, :], ALU.add).then_inc(rows_done, 1)
                    if q == 3:
                        dve.tensor_tensor(ucf, ucf, hs[:, :], ALU.add).then_inc(cols_done, 1)
                        dve.wait_ge(cols_done, n + 1)
                        for r in range(QUARTERS):
                            rows = slot[par][:, QR * r:QR * (r + 1), :]
                            dve.tensor_tensor(rows, rows, u_col[:, :, QR * r:QR * (r + 1)].rearrange("p w h -> p h w"),
                                              ALU.add).then_inc(s_ready, 1)

            run_periods(dve, period, IMAGES)


_INS = ["x", "ln_g", "ln_b", "w_in", "b_in", "conv_w", "conv_b", "a_logit", "ssm_b", "ssm_c", "ssm_d",
        "w_out", "b_out"]


def kernel(**inputs):
    import numpy as _np
    import concourse.bacc as _bacc
    from concourse import mybir as _mybir
    from concourse.bass_utils import run_bass_kernel_spmd as _run

    nc = _bacc.Bacc("TRN2", target_bir_lowering=False, num_devices=1)
    x = inputs["x"]
    tokens = x.shape[1] * x.shape[2]
    given = {n: inputs[n if n == "x" else "L0_conv_" + n] for n in _INS}
    given["ident"] = _np.eye(128, dtype=_np.float32)
    given["steps"] = _np.arange(-1, tokens - 1, dtype=_np.float32).reshape(1, tokens)
    arrays, args = {}, []
    for name, a in given.items():
        a = _np.ascontiguousarray(a)
        arrays[f"in_{name}_dram"] = a
        args.append(nc.dram_tensor(f"in_{name}_dram", a.shape, _mybir.dt.from_np(a.dtype), kind="ExternalInput").ap())
    out = nc.dram_tensor("out_0_dram", x.shape, _mybir.dt.float32, kind="ExternalOutput").ap()
    conv_seq_kernel(nc, *args, out)
    r = _run(nc, [arrays], core_ids=[0])
    return r.results[0]["out_0_dram"]
```

```python
import math
from contextlib import ExitStack

import concourse.bass as bass
from concourse import mybir

F32 = mybir.dt.float32
BF16 = mybir.dt.bfloat16
ALU = mybir.AluOpType
ACT = mybir.ActivationFunctionType

P = 128
A_EPS = 1e-4
POW_MIN = 1e-20
LN_EPS = 1e-5
TINY = 1e-18
QUARTERS = 4
STEPS = 3

PE_TAPS = [(0, 0), (-1, -1), (-1, 1), (1, -1)]
DVE_TAPS = [(1, 0), (-1, 0), (0, -1), (0, 1), (1, 1)]


def finished(g):
    return g + 2


def before(g):
    return g + 1


def run_periods(eng, period, images):
    last = 2 * images - 1
    for n in (-3, -2):
        period(n, n % 2, x=True)
    period(-1, 1, x=True, conv=True)
    for n in (0, 1):
        period(n, n % 2, x=True, conv=True, scan=True)
    for n in (2, 3):
        period(n, n % 2, x=True, conv=True, scan=True, gate=True)
    with eng.Fori(2, images - 2) as pair:
        period(2 * pair, 0, x=True, conv=True, scan=True, gate=True)
        period(2 * pair + 1, 1, x=True, conv=True, scan=True, gate=True)
    period(last - 3, 0, x=True, conv=True, scan=True, gate=True)
    for n in (last - 2, last - 1):
        period(n, n % 2, conv=True, scan=True, gate=True)
    period(last, 1, scan=True, gate=True)
    for n in (last + 1, last + 2):
        period(n, n % 2, gate=True)


def run_steps(eng, half, straight, step):
    if straight:
        for s in range(6 * half, 6 * half + 6):
            step(s, s % 2)
    else:
        with eng.Fori(0, 3) as i:
            for e in range(2):
                step(i * 2 + (6 * half + e), e)


def conv_seq_kernel(nc, x, ln_g, ln_b, w_in, b_in, conv_w, conv_b, a_logit, ssm_b, ssm_c, ssm_d,
                    w_out, b_out, ident_in, steps_in, out):
    IMAGES, HH, WW, D = x.shape
    L = HH * WW
    KH = D // P
    JOB = 3 * P
    TILES = JOB // P
    PER_UNIT = QUARTERS * STEPS
    CH = L // PER_UNIT
    CR = CH // WW
    HALF = PER_UNIT // 2
    SUM_ROWS = [0, HH // 8, HH // 4, HH // 2, 3 * HH // 4, HH]
    PIECES = len(SUM_ROWS) - 1
    IN_ROWS = [0] + [r - 2 for r in SUM_ROWS[1:-1]] + [HH]
    FIRST_CHUNK = [max(0, -((CR - r) // CR)) for r in IN_ROWS[:-1]]
    ROWS = HH + 3
    UNITS = KH * IMAGES
    JOBS = IMAGES * L // JOB
    NT = len(PE_TAPS)
    ND = len(DVE_TAPS)
    LOG_MIN = math.log(POW_MIN)
    assert KH == 2 and L % JOB == 0 and CH == 2 * JOB and CR * WW == CH and JOB == 4 * WW

    x_t = x.rearrange("b h w d -> (b h w) d").rearrange("(g i p) d -> g p i d", i=TILES, p=P)
    out_t = out.rearrange("b h w d -> (b h w) d").rearrange("(g i p) d -> g p i d", i=TILES, p=P)
    xin_d = nc.dram_tensor("xin_scratch", [IMAGES, KH, P, L], F32, kind="Internal").ap()
    s_d = nc.dram_tensor("scan_scratch", [IMAGES, KH, P, L], F32, kind="Internal").ap()
    tab_d = nc.dram_tensor("ratio_scratch", [2, KH, P, L + 2 * CH], F32, kind="Internal").ap()

    ctx = ExitStack()
    with ctx:
        def sb(name, shape, dt=F32):
            return ctx.enter_context(nc.sbuf_tensor(name, shape, dt))

        def ps(name, shape):
            return ctx.enter_context(nc.psum_tensor(name, shape, F32))

        def sem(name):
            return ctx.enter_context(nc.semaphore(name))

        slot = [sb(f"slot{j}", [P, ROWS, WW]) for j in range(KH)]
        slotf = [s[:, :, :].rearrange("p h w -> p (h w)") for s in slot]
        u_col = sb("u_col", [P, WW, HH])
        ucf = u_col[:, :, :].rearrange("p w h -> p (w h)")
        hs = sb("hs", [P, L])
        tab = sb("tab", [P, 2, CH])
        state = sb("state", [P, 2])
        xa = [sb(f"xa{e}", [P, TILES, D]) for e in range(2)]
        xn_x = sb("xn_x", [P, TILES, D])
        xt_x = sb("xt_x", [P, KH, JOB])
        xs = sb("xs", [P, KH, JOB])
        bst = sb("bst", [P, TILES, 6])
        pre = sb("pre", [P, CR, WW])
        xg = [sb(f"xg{e}", [P, TILES, D]) for e in range(2)]
        xn_g = sb("xn_g", [P, TILES, D])
        xt_g = sb("xt_g", [P, KH, JOB])
        y = sb("y", [P, KH, JOB])
        sg = sb("sg", [P, KH, JOB])
        ln_all = sb("ln_all", [P, JOBS, 2 * TILES])
        ln_x = sb("ln_x", [P, 2 * TILES])
        ln_gt = sb("ln_gt", [P, 2 * TILES])
        lt = sb("lt", [P, 4, TILES])
        mhalf = sb("mhalf", [P, TILES])
        w_in_sb = sb("w_in_sb", [P, KH, 2 * D])
        w_out_sb = sb("w_out_sb", [P, KH, D])
        ident = sb("ident", [P, P])
        diag = sb("diag", [P, NT, KH, P])
        cw = sb("cw", [P, 9, KH])
        cols = sb("cols", [P, 10, KH])
        g_c, b_c, bx_c, bg_c, cb_c, al_c, sb_c, sc_c, sd_c, kap = [cols[:, i, :] for i in range(10)]
        more = sb("more", [P, 6, KH])
        a_c, la_c, nla_c, del_c, hbg_c, tmp_c = [more[:, i, :] for i in range(6)]
        bo = sb("bo", [P, D])
        bo_rest = sb("bo_rest", [P, D])
        bo_part = sb("bo_part", [P, D], BF16)
        bo3 = sb("bo3", [P, D], BF16)
        ones3 = sb("ones3", [P, P], BF16)

        ps_x = ps("ps_x", [P, 2, 512])
        ps_g = ps("ps_g", [P, 2, 512])
        ps_c = ps("ps_c", [P, 2, 512])
        ps_o = ps("ps_o", [P, 2, 512])
        ps_of = ps_o[:, :, :].rearrange("p a b -> p (a b)")

        set_in = sem("set_in")
        set_steps = sem("set_steps")
        set_v = sem("set_v")
        set_a = sem("set_a")
        set_done = sem("set_done")
        tab_made = sem("tab_made")
        passed = sem("passed")
        tab_stored = sem("tab_stored")
        x_loaded = [sem(f"x_loaded{e}") for e in range(2)]
        x_stats = sem("x_stats")
        x_norm = sem("x_norm")
        x_turned = sem("x_turned")
        x_evac = sem("x_evac")
        x_proj = sem("x_proj")
        x_out = sem("x_out")
        xin_stored = sem("xin_stored")
        ln_step = sem("ln_step")
        ln_copied = sem("ln_copied")
        xin_loaded = [sem(f"xin_loaded{r}") for r in range(PIECES)]
        conv_summed = sem("conv_summed")
        conv_taken = sem("conv_taken")
        conv_tap = sem("conv_tap")
        silu_done = sem("silu_done")
        conv_out = sem("conv_out")
        tab_loaded = [sem(f"tab_loaded{k}") for k in range(2)]
        scan_f = sem("scan_f")
        scan_b = sem("scan_b")
        ucol_ready = sem("ucol_ready")
        state_saved = sem("state_saved")
        d_added = sem("d_added")
        rows_added = sem("rows_added")
        cols_added = sem("cols_added")
        s_ready = sem("s_ready")
        s_stored = [sem(f"s_stored{r}") for r in range(PIECES)]
        xg_loaded = [sem(f"xg_loaded{e}") for e in range(2)]
        sg_loaded = sem("sg_loaded")
        g_norm = sem("g_norm")
        g_turned = sem("g_turned")
        g_evac = sem("g_evac")
        g_proj = sem("g_proj")
        g_act = sem("g_act")
        y_done = sem("y_done")
        o_proj = sem("o_proj")
        o_added = sem("o_added")
        o_stored = [sem(f"o_stored{e}") for e in range(2)]

        N_IN = 15

        def base(eng, *sems, by=1):
            for s in sems:
                eng.sem_inc(s, by)

        def wait_alone(eng, s, value):
            eng.wait_ge(s, value)
            eng.sem_inc(passed, 1)

        def x_job(n, s):
            return (n + 3) * PER_UNIT + s

        def g_job(n, s):
            return (n - 2) * PER_UNIT + s

        def pair_of(job_of, n, s, e):
            return (job_of(n, 0) // 2 if isinstance(n, int) else
                    (n + (3 if job_of is x_job else -2)) * HALF) + (s - e) // 2

        def tap_done(g, t):
            return g * (ND - 1) + t + 1

        def xin_image(n, par):
            return (n - par) // 2 + par

        def x_image(n, par):
            return (n - par) // 2 + 1 + par

        def g_image(n, par):
            return (n - par) // 2 - 1

        def s_image(n, par):
            return (n - par) // 2 - 1 + par

        block = ctx.enter_context(nc.Block())

        @block.sync
        def _(sp):
            def col(v, width=KH):
                return v.rearrange("(j p) -> p j", p=P)

            with nc.allow_non_contiguous_dma(reason="small per-channel vectors, once"):
                sp.dma_start(w_in_sb[:, :, :], w_in.rearrange("(k p) n -> p k n", p=P)).then_inc(set_in, 16)
                sp.dma_start(w_out_sb[:, :, :], w_out.rearrange("(k p) n -> p k n", p=P)).then_inc(set_in, 16)
                sp.dma_start(ident[:, :], ident_in).then_inc(set_in, 16)
                for dst, src in ((g_c, col(ln_g)), (b_c, col(ln_b)), (cb_c, col(conv_b)), (al_c, col(a_logit)),
                                 (sb_c, col(ssm_b)), (sc_c, col(ssm_c)), (sd_c, col(ssm_d)),
                                 (bx_c, col(b_in[0:D])), (bg_c, col(b_in[D:2 * D]))):
                    sp.dma_start(dst, src).then_inc(set_in, 16)
                cwv = conv_w.rearrange("a b o (j p) -> p (a b o) j", p=P)
                for j in range(KH):
                    sp.dma_start(cw[:, :, j], cwv[:, :, j]).then_inc(set_in, 16)
                sp.dma_start(bo[:, :], b_out.rearrange("(o d) -> o d", o=1).broadcast_to([P, D])).then_inc(set_in, 16)
                sp.dma_start(ucf, steps_in.broadcast_to([P, L])).then_inc(set_steps, 16)
            base(sp, xin_stored, *o_stored, by=16)

            def load_x(g, e, pair):
                sp.dma_start(xa[e][:, :, :], x_t[bass.ds(g, 1)].rearrange("o p i d -> (o p) i d")
                             ).then_inc(x_loaded[e], 16)

            def load_xg(g, e):
                sp.dma_start(xg[e][:, :, :], x_t[bass.ds(g, 1)].rearrange("o p i d -> (o p) i d")
                             ).then_inc(xg_loaded[e], 16)

            load_x(0, 0, 0)
            for j in range(KH):
                sp.wait_ge(tab_made, j + 1)
                for h in range(2):
                    sp.dma_start(tab_d[h, j, :, 0:L], hs[:, :]).then_inc(tab_stored, 16)
                    k = j if h == 0 else 1 - j
                    sp.dma_start(tab_d[h, k, :, L:L + 2 * CH], hs[:, 0:2 * CH]).then_inc(tab_stored, 16)
                sp.wait_ge(tab_stored, 64 * (j + 1))
            for k in range(2):
                sp.dma_start(tab[:, k, :], tab_d[0, 0, :, k * CH:(k + 1) * CH]).then_inc(tab_loaded[k], 16)

            def period(n, par, x=False, conv=False, scan=False, gate=False):
                static = isinstance(n, int)
                final_x = static and x and n == UNITS - 4
                final_g = static and gate and n == UNITS + 1

                def store_sums(r):
                    if r == 0:
                        wait_alone(sp, s_ready, n)
                    lo, hi = WW * SUM_ROWS[r], WW * SUM_ROWS[r + 1]
                    sp.dma_start(s_d[s_image(n, par), 1 - par, :, lo:hi], slotf[1 - par][:, lo:hi]
                                 ).then_inc(s_stored[r], 16)

                def load_conv_input(r):
                    jobs = (xin_image(n, par) + 1) * (L // JOB)
                    if r == 0:
                        wait_alone(sp, xin_stored, (jobs - L // JOB // 2) * 16 + 16)
                    elif IN_ROWS[r + 1] > HH // 2 >= IN_ROWS[r]:
                        wait_alone(sp, xin_stored, jobs * 16 + 16)
                    if not static or n >= 1:
                        wait_alone(sp, s_stored[r], n * 16)
                    sp.dma_start(slot[1 - par][:, 2 + IN_ROWS[r]:2 + IN_ROWS[r + 1], :].rearrange("p h w -> p (h w)"),
                                 xin_d[xin_image(n, par), 1 - par, :, WW * IN_ROWS[r]:WW * IN_ROWS[r + 1]]
                                 ).then_inc(xin_loaded[r], 16)

                storing = (scan or gate) and (not static or 1 <= n <= UNITS)

                def step(s, e):
                    fixed = isinstance(s, int)
                    half = s // HALF if fixed else 1
                    if storing and fixed and s == 0:
                        store_sums(0)
                        store_sums(1)
                    if x and not (final_x and s == PER_UNIT - 1):
                        g = x_job(n, s) + 1
                        wait_alone(sp, x_norm, g)
                        load_x(g, 1 - e, None)
                    if conv and fixed and s == 1:
                        load_conv_input(1)
                    if gate:
                        g = g_job(n, s)
                        if fixed and par == 0 and s in (0, HALF // 2):
                            wait_alone(sp, s_stored[s // (HALF // 2)], n * 16)
                        wait_alone(sp, y_done, before(g))
                        sp.dma_start(sg[:, :, :],
                                     s_d[g_image(n, par)][:, :, bass.ds((s + par * PER_UNIT) * JOB, JOB)]
                                     .rearrange("k p t -> p k t")).then_inc(sg_loaded, 16)
                    if conv and fixed and s == 0:
                        load_conv_input(0)
                    if storing and fixed and s < 3:
                        store_sums(s + 2)
                    if gate and not (final_g and s == PER_UNIT - 1):
                        g = g_job(n, s) + 1
                        wait_alone(sp, o_stored[1 - e], (pair_of(g_job, n, s, e) + e) * 16 + 16)
                        load_xg(g, 1 - e)
                    if conv and fixed and s in (1, 2, 3):
                        load_conv_input(s + 1)
                    if scan:
                        for k in range(2):
                            pr = n * (2 * PER_UNIT) + (s * 2 + (2 + k))
                            wait_alone(sp, scan_b, pr + 1)
                            sp.dma_start(tab[:, k, :],
                                         tab_d[half, par, :, bass.ds((s * 2 + (2 + k - PER_UNIT * half)) * CH, CH)]
                                         ).then_inc(tab_loaded[k], 16)

                if gate and static and n == 2:
                    load_xg(0, 0)
                run_steps(sp, 0, True, step)
                if gate and par == 0:
                    for r in range(2, PIECES):
                        wait_alone(sp, s_stored[r], n * 16)
                run_steps(sp, 1, final_x or final_g, step)

            run_periods(sp, period, IMAGES)
            for r in range(PIECES):
                sp.wait_ge(s_stored[r], 16 * UNITS)
            for k in range(2):
                sp.wait_ge(tab_loaded[k], 16 * (UNITS * PER_UNIT + 1))
            sp.wait_ge(xin_stored, 16 * (JOBS + 1))
            for e in range(2):
                sp.wait_ge(o_stored[e], 16 * (JOBS // 2 + 1))

        @block.tensor
        def _(pe):
            base(pe, x_turned, x_proj, g_turned, g_proj, o_proj, conv_summed)
            pe.wait_ge(set_done, 1)

            def turn(ps_t, src, done):
                for t in range(TILES):
                    for k in range(KH):
                        ins = pe.transpose(ps_t[:, k, t * P:(t + 1) * P], src[:, t, k * P:(k + 1) * P], ident[:, :])
                ins.then_inc(done, 1)

            def project(ps_t, src, first, done):
                for j in range(KH):
                    for k in range(KH):
                        ins = pe.matmul(ps_t[:, j, 0:JOB], w_in_sb[:, k, first + j * P:first + (j + 1) * P],
                                        src[:, k, :], start=(k == 0), stop=(k == KH - 1))
                ins.then_inc(done, 1)

            def conv_taps(j, s, g, parts):
                if 0 in parts:
                    pe.wait_ge(conv_taken, before(g))
                hr = CR // 2
                for r in parts:
                    acc = ps_c[:, r, 0:JOB].rearrange("p (h w) -> p h w", w=WW)
                    for t, (dh, dw) in enumerate(PE_TAPS):
                        lo, hi = max(0, -dw), WW - max(0, dw)
                        top = 1 if isinstance(s, int) and s == 0 and r == 0 and dh < 0 else 0
                        ins = pe.matmul(acc[:, top:hr, lo:hi], diag[:, t, j, :],
                                        slot[j][:, bass.ds(s * CR + (hr * r + 2 + dh + top), hr - top), lo + dw:hi + dw],
                                        start=(t == 0), stop=(t == NT - 1))
                if 1 in parts:
                    ins.then_inc(conv_summed, 1)

            def period(n, par, x=False, conv=False, scan=False, gate=False):
                def step(s, e):
                    gx, gg, gc = x_job(n, s), g_job(n, s), (n + 1) * PER_UNIT + s
                    if gate:
                        pe.wait_ge(g_norm, finished(gg))
                        pe.wait_ge(g_act, before(gg))
                        turn(ps_g, xn_g, g_turned)
                    if x:
                        pe.wait_ge(x_norm, finished(gx))
                        pe.wait_ge(x_out, before(gx))
                        turn(ps_x, xn_x, x_turned)
                    early = not (isinstance(s, int) and s == 0)
                    if conv and early:
                        if isinstance(s, int) and s in FIRST_CHUNK:
                            pe.wait_ge(xin_loaded[FIRST_CHUNK.index(s)], (n + 1) * 16 + 16)
                        conv_taps(1 - par, s, gc, (0,))
                    if gate:
                        pe.wait_ge(g_evac, finished(gg))
                        project(ps_g, xt_g, D, g_proj)
                    if conv and early:
                        conv_taps(1 - par, s, gc, (1,))
                    if x:
                        pe.wait_ge(x_evac, finished(gx))
                        project(ps_x, xt_x, 0, x_proj)
                    if conv and not early:
                        pe.wait_ge(xin_loaded[0], (n + 1) * 16 + 16)
                        conv_taps(1 - par, s, gc, (0, 1))
                    if gate:
                        pe.wait_ge(y_done, finished(gg))
                        pe.wait_ge(o_added, before(gg))
                        for t in range(TILES):
                            o = ps_of[:, t * D:(t + 1) * D]
                            pe.matmul(o, ones3[:, :], bo3[:, :], start=True, stop=False)
                            for k in range(KH):
                                ins = pe.matmul(o, y[:, k, t * P:(t + 1) * P], w_out_sb[:, k, :],
                                                start=False, stop=(k == KH - 1))
                        ins.then_inc(o_proj, 1)

                run_steps(pe, 0, True, step)
                if conv:
                    wait_alone(pe, xin_loaded[PIECES - 1], (n + 1) * 16 + 16)
                run_steps(pe, 1, False, step)

            run_periods(pe, period, IMAGES)

        @block.scalar
        def _(act):
            base(act, x_evac, x_out, g_evac, g_act, conv_out, silu_done)
            act.wait_ge(set_in, 16 * N_IN)
            act.activation(tmp_c, al_c, ACT.Exp, scale=-1.0).then_inc(set_a, 1)
            act.wait_ge(set_v, 3)
            act.activation(la_c, a_c, ACT.Ln).then_inc(set_a, 1)
            for j in range(KH):
                act.wait_ge(set_v, 6 + 2 * j)
                act.activation(hs[:, :], hs[:, :], ACT.Exp).then_inc(set_a, 1)
            act.wait_ge(set_done, 1)

            def silu(j, s, g):
                act.wait_ge(conv_tap, tap_done(g, ND - 1))
                act.activation(pre[:, :, :], pre[:, :, :], ACT.Silu, bias=cb_c[:, j:j + 1]).then_inc(silu_done, 1)
                act.wait_ge(silu_done, finished(g))
                act.activation(slot[j][:, bass.ds(s * CR, CR), :], pre[:, :, :], ACT.Copy,
                               scale=kap[:, j:j + 1]).then_inc(conv_out, 1)

            def store_out(g, e):
                wait_alone(act, o_added, finished(g))
                act.dma_start(out_t[bass.ds(g, 1)].rearrange("o p i d -> (o p) i d"), xg[e][:, :, :]
                              ).then_inc(o_stored[e], 16)

            def period(n, par, x=False, conv=False, scan=False, gate=False):
                static = isinstance(n, int)

                def step(s, e):
                    fixed = isinstance(s, int)
                    gx, gg, gc = x_job(n, s), g_job(n, s), (n + 1) * PER_UNIT + s
                    if scan and fixed and s == 0:
                        silu(par, PER_UNIT - 1, gc - 1)
                    if gate:
                        act.wait_ge(g_turned, finished(gg))
                        act.wait_ge(g_proj, before(gg))
                        for k in range(KH):
                            ins = act.activation(xt_g[:, k, :], ps_g[:, k, 0:JOB], ACT.Identity,
                                                 bias=b_c[:, k:k + 1], scale=g_c[:, k:k + 1])
                        ins.then_inc(g_evac, 1)
                    if x:
                        act.wait_ge(x_turned, finished(gx))
                        act.wait_ge(x_proj, before(gx))
                        for k in range(KH):
                            ins = act.activation(xt_x[:, k, :], ps_x[:, k, 0:JOB], ACT.Identity,
                                                 bias=b_c[:, k:k + 1], scale=g_c[:, k:k + 1])
                        ins.then_inc(x_evac, 1)
                    if gate and not (static and n == 2 and fixed and s == 0):
                        store_out(gg - 1, 1 - e)
                    if conv and not (fixed and s == 0):
                        silu(1 - par, s - 1, gc - 1)
                    if gate:
                        act.wait_ge(g_proj, finished(gg))
                        act.wait_ge(o_proj, before(gg))
                        for j in range(KH):
                            ins = act.activation(y[:, j, :], ps_g[:, j, 0:JOB], ACT.Tanh,
                                                 bias=hbg_c[:, j:j + 1], scale=0.5)
                        ins.then_inc(g_act, 1)
                    if x:
                        act.wait_ge(x_proj, finished(gx))
                        act.wait_ge(xin_stored, gx * 16 + 16)
                        for j in range(KH):
                            ins = act.activation(xs[:, j, :], ps_x[:, j, 0:JOB], ACT.Identity,
                                                 bias=bx_c[:, j:j + 1])
                        ins.then_inc(x_out, 1)
                        wait_alone(act, x_out, finished(gx))
                        act.dma_start(xin_d[x_image(n, par)][:, :, bass.ds((s + (1 - par) * PER_UNIT) * JOB, JOB)]
                                      .rearrange("k p t -> p k t"), xs[:, :, :]).then_inc(xin_stored, 16)
                    if scan and fixed and s < STEPS:
                        if s == 0:
                            act.wait_ge(conv_out, finished(n * PER_UNIT + (PER_UNIT - 1)))
                            if not static or n >= 1:
                                act.wait_ge(s_ready, n)
                        R = HH // STEPS
                        act.activation(u_col[:, :, R * s:R * (s + 1)].rearrange("p w h -> p h w"),
                                       slot[par][:, R * s:R * (s + 1), :], ACT.Copy).then_inc(ucol_ready, 1)

                run_steps(act, 0, True, step)
                run_steps(act, 1, False, step)

            run_periods(act, period, IMAGES)
            store_out(JOBS - 1, 1)

        @block.gpsimd
        def _(pool):
            base(pool, x_norm, g_norm, ln_step)
            pool.memset(mhalf[:, :], -0.5).then_inc(ln_step, 1)
            LN_OPS = 10

            def period(n, par, x=False, conv=False, scan=False, gate=False):
                def step(s, e):
                    if x:
                        g = x_job(n, s)
                        c = g * LN_OPS + 2
                        pool.wait_ge(x_stats, finished(g))
                        pool.wait_ge(ln_step, c)
                        pool.tensor_tensor(lt[:, 0, :], bst[:, :, 1], bst[:, :, 4], ALU.add).then_inc(ln_step, 1)
                        pool.tensor_tensor(lt[:, 1, :], bst[:, :, 1], bst[:, :, 4], ALU.subtract).then_inc(ln_step, 1)
                        pool.tensor_tensor(lt[:, 2, :], bst[:, :, 2], bst[:, :, 5], ALU.add).then_inc(ln_step, 1)
                        pool.wait_ge(ln_step, c + 3)
                        pool.tensor_tensor(lt[:, 1, :], lt[:, 1, :], lt[:, 1, :], ALU.mult).then_inc(ln_step, 1)
                        wait_alone(pool, ln_step, c + 4)
                        pool.tensor_scalar(lt[:, 1, :], lt[:, 1, :], D / 4.0, 0.0, ALU.mult, ALU.add).then_inc(ln_step, 1)
                        pool.wait_ge(ln_step, c + 5)
                        pool.tensor_tensor(lt[:, 2, :], lt[:, 1, :], lt[:, 2, :], ALU.add).then_inc(ln_step, 1)
                        wait_alone(pool, ln_step, c + 6)
                        pool.tensor_scalar(lt[:, 2, :], lt[:, 2, :], 1.0 / D, LN_EPS, ALU.mult, ALU.add).then_inc(ln_step, 1)
                        pool.wait_ge(ln_step, c + 7)
                        pool.tensor_tensor(ln_x[:, 0:TILES], lt[:, 2, :], mhalf[:, :], ALU.pow).then_inc(ln_step, 1)
                        pool.tensor_scalar(lt[:, 0, :], lt[:, 0, :], -0.5, 0.0, ALU.mult, ALU.add).then_inc(ln_step, 1)
                        pool.wait_ge(ln_step, c + 9)
                        pool.tensor_tensor(ln_x[:, TILES:2 * TILES], lt[:, 0, :], ln_x[:, 0:TILES], ALU.mult).then_inc(ln_step, 1)
                        pool.wait_ge(ln_step, c + 10)
                        pool.tensor_copy(ln_all[:, bass.ds(g, 1), :].rearrange("p o t -> p (o t)"), ln_x[:, :])
                        wait_alone(pool, x_turned, before(g))
                        for t in range(TILES):
                            ins = pool.tensor_scalar(xn_x[:, t, :], xa[e][:, t, :], ln_x[:, t:t + 1],
                                                     ln_x[:, TILES + t:TILES + t + 1], ALU.mult, ALU.add)
                        ins.then_inc(x_norm, 1)
                    if gate:
                        g = g_job(n, s)
                        pool.wait_ge(g_norm, before(g))
                        pool.tensor_copy(ln_gt[:, :], ln_all[:, bass.ds(g, 1), :].rearrange("p o t -> p (o t)")
                                         ).then_inc(ln_copied, 1)
                        pool.wait_ge(ln_copied, g + 1)
                        pool.wait_ge(xg_loaded[e], pair_of(g_job, n, s, e) * 16 + 16)
                        wait_alone(pool, g_turned, before(g))
                        for t in range(TILES):
                            ins = pool.tensor_scalar(xn_g[:, t, :], xg[e][:, t, :], ln_gt[:, t:t + 1],
                                                     ln_gt[:, TILES + t:TILES + t + 1], ALU.mult, ALU.add)
                        ins.then_inc(g_norm, 1)

                for half in range(2):
                    run_steps(pool, half, False, step)

            run_periods(pool, period, IMAGES)

        @block.vector
        def _(dve):
            base(dve, x_stats, conv_taken, conv_tap, scan_f, y_done, o_added)
            base(dve, scan_b, by=2)
            for j in range(KH):
                dve.memset(slot[j][:, ROWS - 1, :], 0.0)
            dve.memset(ones3[:, :], 1.0)

            dve.wait_ge(set_a, 1)
            dve.tensor_scalar(tmp_c, tmp_c, 1.0, None, ALU.add).then_inc(set_v, 1)
            dve.wait_ge(set_v, 1)
            dve.reciprocal(tmp_c, tmp_c).then_inc(set_v, 1)
            dve.wait_ge(set_v, 2)
            dve.tensor_scalar(a_c, tmp_c, A_EPS, 1.0 - A_EPS, ALU.max, ALU.min).then_inc(set_v, 1)
            dve.wait_ge(set_a, 2)
            dve.tensor_scalar(nla_c, la_c, -1.0, None, ALU.mult).then_inc(set_v, 1)
            dve.wait_ge(set_v, 4)
            dve.wait_ge(set_steps, 16)
            for j in range(KH):
                if j:
                    dve.wait_ge(tab_stored, 64 * j)
                dve.tensor_scalar(hs[:, :], ucf, nla_c[:, j:j + 1], LOG_MIN, ALU.mult, ALU.add).then_inc(set_v, 1)
                dve.wait_ge(set_v, 5 + 2 * j)
                dve.tensor_scalar(hs[:, :], hs[:, :], 0.0, None, ALU.min).then_inc(set_v, 1)
                dve.wait_ge(set_a, 3 + j)
                dve.tensor_scalar(hs[:, :], hs[:, :], 1.0, a_c[:, j:j + 1], ALU.min, ALU.max).then_inc(tab_made, 1)

            dve.wait_ge(set_in, 16 * N_IN)
            dve.tensor_tensor(tmp_c, sb_c, sc_c, ALU.mult).then_inc(set_v, 1)
            dve.wait_ge(set_v, 9)
            dve.tensor_scalar(kap, tmp_c, 0.125, None, ALU.mult).then_inc(set_v, 1)
            dve.wait_ge(set_v, 10)
            dve.tensor_tensor(tmp_c, kap, kap, ALU.mult).then_inc(set_v, 1)
            dve.wait_ge(set_v, 11)
            dve.tensor_scalar(tmp_c, tmp_c, TINY * TINY, 2.0 * TINY, ALU.is_lt, ALU.mult).then_inc(set_v, 1)
            dve.wait_ge(set_v, 12)
            dve.tensor_tensor(kap, kap, tmp_c, ALU.add).then_inc(set_v, 1)
            dve.wait_ge(set_v, 13)
            dve.reciprocal(tmp_c, kap).then_inc(set_v, 1)
            dve.wait_ge(set_v, 14)
            dve.scalar_tensor_tensor(out=del_c, in0=sd_c, scalar=0.5, in1=tmp_c, op0=ALU.mult, op1=ALU.mult
                                     ).then_inc(set_v, 1)
            dve.tensor_scalar(hbg_c, bg_c, 0.5, None, ALU.mult).then_inc(set_v, 1)
            for t, (dh, dw) in enumerate(PE_TAPS):
                tap = (dh + 1) * 3 + dw + 1
                for j in range(KH):
                    dve.tensor_scalar(diag[:, t, j, :], ident[:, :], cw[:, tap, j:j + 1], None, ALU.mult)
            dve.tensor_copy(bo_part[:, :], bo[:, :]).then_inc(set_v, 1)
            dve.wait_ge(set_v, 17)
            dve.tensor_tensor(bo_rest[:, :], bo[:, :], bo_part[:, :], ALU.subtract).then_inc(set_v, 1)
            dve.tensor_scalar(bo3[:, :], bo_part[:, :], ident[:, 0:1], None, ALU.mult).then_inc(set_v, 1)
            for r in range(1, 3):
                dve.wait_ge(set_v, 19 + 3 * (r - 1))
                dve.tensor_copy(bo_part[:, :], bo_rest[:, :]).then_inc(set_v, 1)
                dve.wait_ge(set_v, 20 + 3 * (r - 1))
                dve.tensor_tensor(bo_rest[:, :], bo_rest[:, :], bo_part[:, :], ALU.subtract).then_inc(set_v, 1)
                dve.scalar_tensor_tensor(out=bo3[:, :], in0=bo_part[:, :], scalar=ident[:, r:r + 1], in1=bo3[:, :],
                                         op0=ALU.mult, op1=ALU.add).then_inc(set_v, 1)
            dve.wait_ge(set_v, 25)
            dve.memset(state[:, :], 0.0).then_inc(set_done, 1)

            def stats(g, e, pair):
                dve.wait_ge(x_loaded[e], pair * 16 + 16)
                dve.wait_ge(x_norm, before(g))
                for t in range(TILES):
                    ins = dve.bn_stats(bst[:, t, :], xa[e][:, t, :])
                ins.then_inc(x_stats, 1)

            def tap(j, s, g, t):
                dh, dw = DVE_TAPS[t]
                w = cw[:, (dh + 1) * 3 + dw + 1, j:j + 1]
                top = 1 if isinstance(s, int) and s == 0 and dh < 0 else 0
                src = slot[j][:, bass.ds(s * CR + (2 + dh + top), CR - top), :]
                if t == 0:
                    dve.wait_ge(conv_summed, finished(g))
                    dve.wait_ge(conv_out, before(g))
                    dve.scalar_tensor_tensor(
                        out=pre[:, :, :].rearrange("p (a h) w -> p a (h w)", a=2),
                        in0=src.rearrange("p (a h) w -> p a (h w)", a=2), scalar=w,
                        in1=ps_c[:, :, 0:JOB], op0=ALU.mult, op1=ALU.add).then_inc(conv_taken, 1)
                    return
                lo, hi = max(0, -dw), WW - max(0, dw)
                if t == 1:
                    dve.wait_ge(conv_taken, finished(g))
                else:
                    dve.wait_ge(conv_tap, tap_done(g, t - 1))
                dve.scalar_tensor_tensor(
                    out=pre[:, top:CR, lo:hi], in0=src[:, :, lo + dw:hi + dw], scalar=w,
                    in1=pre[:, top:CR, lo:hi], op0=ALU.mult, op1=ALU.add).then_inc(conv_tap, 1)

            def forward(n, src, phase, c):
                pr = n * (2 * PER_UNIT) + (PER_UNIT * phase + c)
                lo = c * CH
                dve.wait_ge(tab_loaded[c % 2], (n * PER_UNIT + (HALF * phase + c // 2)) * 16 + 16)
                dve.wait_ge(scan_f, before(pr))
                if c == 0:
                    init = 0.0
                elif c < HALF or (c == HALF and phase == 1):
                    init = hs[:, lo - 1:lo]
                elif c == HALF:
                    init = state[:, 0:1]
                else:
                    init = src[:, lo - 1:lo]
                dst = hs[:, lo:lo + CH] if c < HALF else src[:, lo:lo + CH]
                dve.tensor_tensor_scan(dst, tab[:, c % 2, :], src[:, lo:lo + CH], init, ALU.mult, ALU.add
                                       ).then_inc(scan_f, 1)

            def backward(n, src, phase, c):
                pr = n * (2 * PER_UNIT) + (PER_UNIT * phase + c)
                lo = L - (c + 1) * CH
                hi = lo + CH
                dve.wait_ge(scan_b, pr + 2)
                if c == 0:
                    init = 0.0
                elif c < HALF or (c == HALF and phase == 1):
                    init = hs[:, hi:hi + 1]
                elif c == HALF:
                    init = state[:, 1:2]
                else:
                    init = src[:, hi:hi + 1]
                flip = slice(hi - 1, lo - 1 if lo else None, -1)
                dst = hs[:, flip] if c < HALF else src[:, flip]
                dve.tensor_tensor_scan(dst, tab[:, c % 2, :], src[:, flip], init, ALU.mult, ALU.add
                                       ).then_inc(scan_b, 1)

            def add(n, par, q, c):
                u = slotf[par]
                lo = c * CH
                uv, hv = u[:, lo:lo + CH], hs[:, lo:lo + CH]
                if q == 0:
                    dve.scalar_tensor_tensor(out=hv, in0=uv, scalar=del_c[:, par:par + 1], in1=hv,
                                             op0=ALU.mult, op1=ALU.add).then_inc(d_added, 1)
                elif q == 1:
                    dve.tensor_tensor(uv, uv, hv, ALU.add).then_inc(rows_added, 1)
                else:
                    src = hs[:, lo:lo + CH].rearrange("p (w h) -> p h w", h=HH) if q == 2 else \
                        u_col[:, c * CR:(c + 1) * CR, :].rearrange("p w h -> p h w")
                    dst = slot[par][:, 0:HH, c * CR:(c + 1) * CR]
                    dve.tensor_tensor(dst, dst, src, ALU.add).then_inc(cols_added, 1)

            def settle_states(n):
                if not isinstance(n, int) or n >= 1:
                    dve.wait_ge(s_ready, n)
                pairs = n * (2 * PER_UNIT) + HALF
                dve.wait_ge(scan_f, pairs + 1)
                dve.wait_ge(scan_b, pairs + 2)
                dve.tensor_copy(state[:, 0:1], hs[:, L // 2 - 1:L // 2]).then_inc(state_saved, 1)
                dve.tensor_copy(state[:, 1:2], hs[:, L // 2:L // 2 + 1]).then_inc(state_saved, 1)

            def period(n, par, x=False, conv=False, scan=False, gate=False):
                static = isinstance(n, int)
                final_x = static and x and n == UNITS - 4
                final_g = static and gate and n == UNITS + 1

                def add_residual(g, e):
                    dve.wait_ge(o_proj, finished(g))
                    xv = xg[e][:, :, :].rearrange("p t d -> p (t d)")
                    dve.tensor_tensor(xv, ps_of[:, 0:TILES * D], xv, ALU.add).then_inc(o_added, 1)

                def pair_scans(s, k):
                    q = s // STEPS
                    phase, c = q // 2, HALF * (q % 2) + 2 * (s % STEPS) + k
                    src = slotf[par] if phase == 0 else ucf
                    ops = []
                    if c == HALF and q == 1:
                        settle_states(n)
                        dve.wait_ge(state_saved, 2 * n + 2)
                        add(n, par, 0, c - 1)
                        add(n, par, 0, PER_UNIT - c)
                        dve.wait_ge(d_added, (n + 1) * PER_UNIT)
                        dve.wait_ge(ucol_ready, (n + 1) * STEPS)
                    if c == 0 and q == 2:
                        dve.wait_ge(scan_f, before(n * (2 * PER_UNIT) + PER_UNIT))
                        dve.wait_ge(scan_b, n * (2 * PER_UNIT) + (PER_UNIT + 2))
                        add(n, par, 1, PER_UNIT - 1)
                        add(n, par, 1, 0)
                        dve.wait_ge(rows_added, (n + 1) * PER_UNIT)
                    forward(n, src, phase, c)
                    backward(n, src, phase, c)

                def pair_adds(s, k):
                    q = s // STEPS
                    phase, c = q // 2, HALF * (q % 2) + 2 * (s % STEPS) + k
                    if c == 0 or (c == HALF and q == 1):
                        return
                    qq = 2 if (q == 3 and c == HALF) else q
                    if q == 3 and c == HALF + 1:
                        dve.wait_ge(cols_added, n * (2 * PER_UNIT) + PER_UNIT)
                    pr = n * (2 * PER_UNIT) + (PER_UNIT * phase + c)
                    dve.wait_ge(scan_f, finished(pr))
                    add(n, par, qq, c - 1)
                    dve.wait_ge(scan_b, pr + 3)
                    add(n, par, qq, PER_UNIT - c)

                def step(s, e):
                    gx, gg, gc = x_job(n, s), g_job(n, s), (n + 1) * PER_UNIT + s
                    if gate and not (static and n == 2 and isinstance(s, int) and s == 0):
                        add_residual(gg - 1, 1 - e)
                    if x and not (final_x and s == PER_UNIT - 1):
                        stats(gx + 1, 1 - e, pair_of(x_job, n, s, e) + e)
                    if scan:
                        if s == 0:
                            dve.wait_ge(conv_out, finished(n * PER_UNIT + (PER_UNIT - 1)))
                        pair_scans(s, 0)
                        pair_adds(s, 0)
                        pair_scans(s, 1)
                    if gate:
                        dve.wait_ge(g_act, finished(gg))
                        dve.wait_ge(sg_loaded, gg * 16 + 16)
                        dve.scalar_tensor_tensor(out=y[:, :, :], in0=y[:, :, :], scalar=1.0, in1=sg[:, :, :],
                                                 op0=ALU.add, op1=ALU.mult).then_inc(y_done, 1)
                    if scan:
                        pair_adds(s, 1)
                    if conv:
                        for t in range(ND):
                            tap(1 - par, s, gc, t)

                run_steps(dve, 0, scan or conv, step)
                run_steps(dve, 1, scan or conv, step)
                if final_g:
                    add_residual(JOBS - 1, 1)
                if scan:
                    dve.wait_ge(scan_f, before(n * (2 * PER_UNIT) + 2 * PER_UNIT))
                    dve.wait_ge(scan_b, n * (2 * PER_UNIT) + (2 * PER_UNIT + 2))
                    add(n, par, 3, PER_UNIT - 1)
                    add(n, par, 3, 0)
                    dve.wait_ge(cols_added, (n + 1) * (2 * PER_UNIT))
                    dve.memset(state[:, :], 0.0).then_inc(s_ready, 1)

            dve.wait_ge(set_done, 1)
            stats(0, 0, 0)
            run_periods(dve, period, IMAGES)


_INS = ["x", "ln_g", "ln_b", "w_in", "b_in", "conv_w", "conv_b", "a_logit", "ssm_b", "ssm_c", "ssm_d",
        "w_out", "b_out"]


def kernel(**inputs):
    import numpy as _np
    import concourse.bacc as _bacc
    from concourse import mybir as _mybir
    from concourse.bass_utils import run_bass_kernel_spmd as _run

    nc = _bacc.Bacc("TRN2", target_bir_lowering=False, num_devices=1)
    x = inputs["x"]
    tokens = x.shape[1] * x.shape[2]
    given = {n: inputs[n if n == "x" else "L0_conv_" + n] for n in _INS}
    given["ident"] = _np.eye(128, dtype=_np.float32)
    given["steps"] = _np.arange(-1, tokens - 1, dtype=_np.float32).reshape(1, tokens)
    arrays, args = {}, []
    for name, a in given.items():
        a = _np.ascontiguousarray(a)
        arrays[f"in_{name}_dram"] = a
        args.append(nc.dram_tensor(f"in_{name}_dram", a.shape, _mybir.dt.from_np(a.dtype), kind="ExternalInput").ap())
    out = nc.dram_tensor("out_0_dram", x.shape, _mybir.dt.float32, kind="ExternalOutput").ap()
    conv_seq_kernel(nc, *args, out)
    r = _run(nc, [arrays], core_ids=[0])
    return r.results[0]["out_0_dram"]
```

```python
import math
from contextlib import ExitStack

import concourse.bass as bass
from concourse import mybir

F32 = mybir.dt.float32
BF16 = mybir.dt.bfloat16
ALU = mybir.AluOpType
ACT = mybir.ActivationFunctionType

P = 128
A_EPS = 1e-4
POW_MIN = 1e-20
LN_EPS = 1e-5
TINY = 1e-18
QUARTERS = 4
STEPS = 3

PE_TAPS = [(0, 0), (-1, -1), (-1, 1), (1, -1)]
DVE_TAPS = [(1, 0), (-1, 0), (0, -1), (0, 1), (1, 1)]


def finished(g):
    return g + 2


def before(g):
    return g + 1


def run_periods(eng, period, images):
    last = 2 * images - 1
    for n in (-3, -2):
        period(n, n % 2, x=True)
    period(-1, 1, x=True, conv=True)
    for n in (0, 1):
        period(n, n % 2, x=True, conv=True, scan=True)
    for n in (2, 3):
        period(n, n % 2, x=True, conv=True, scan=True, gate=True)
    with eng.Fori(2, images - 2) as pair:
        period(2 * pair, 0, x=True, conv=True, scan=True, gate=True)
        period(2 * pair + 1, 1, x=True, conv=True, scan=True, gate=True)
    period(last - 3, 0, x=True, conv=True, scan=True, gate=True)
    for n in (last - 2, last - 1):
        period(n, n % 2, conv=True, scan=True, gate=True)
    period(last, 1, scan=True, gate=True)
    for n in (last + 1, last + 2):
        period(n, n % 2, gate=True)


def run_steps(eng, half, straight, step):
    if straight:
        for s in range(6 * half, 6 * half + 6):
            step(s, s % 2)
    else:
        with eng.Fori(0, 3) as i:
            for e in range(2):
                step(i * 2 + (6 * half + e), e)


def conv_seq_kernel(nc, x, ln_g, ln_b, w_in, b_in, conv_w, conv_b, a_logit, ssm_b, ssm_c, ssm_d,
                    w_out, b_out, ident_in, steps_in, out):
    IMAGES, HH, WW, D = x.shape
    L = HH * WW
    KH = D // P
    JOB = 3 * P
    TILES = JOB // P
    PER_UNIT = QUARTERS * STEPS
    CH = L // PER_UNIT
    CR = CH // WW
    HALF = PER_UNIT // 2
    SUM_ROWS = [HH * r // 8 for r in (0, 1, 2, 3, 4, 5, 6, 8)]
    PIECES = len(SUM_ROWS) - 1
    IN_ROWS = [0] + [r - 2 for r in SUM_ROWS[1:-1]] + [HH]
    FIRST_CHUNK = [max(1, -((CR - r) // CR)) for r in IN_ROWS[:-1]]
    HEAD = (HALF - 1) * CH
    ROWS = HH + 3
    UNITS = KH * IMAGES
    JOBS = IMAGES * L // JOB
    NT = len(PE_TAPS)
    ND = len(DVE_TAPS)
    LOG_MIN = math.log(POW_MIN)
    PARTS = HALF
    TP = L // PARTS
    assert KH == 2 and L % JOB == 0 and CH == 2 * JOB and CR * WW == CH and JOB == 4 * WW

    x_t = x.rearrange("b h w d -> (b h w) d").rearrange("(g i p) d -> g p i d", i=TILES, p=P)
    out_t = out.rearrange("b h w d -> (b h w) d").rearrange("(g i p) d -> g p i d", i=TILES, p=P)
    xin_d = nc.dram_tensor("xin_scratch", [IMAGES, KH, P, L], F32, kind="Internal").ap()
    s_d = nc.dram_tensor("scan_scratch", [IMAGES, KH, P, L], F32, kind="Internal").ap()
    tab_d = nc.dram_tensor("ratio_scratch", [2, KH, P, L + 2 * CH], F32, kind="Internal").ap()

    ctx = ExitStack()
    with ctx:
        def sb(name, shape, dt=F32):
            return ctx.enter_context(nc.sbuf_tensor(name, shape, dt))

        def ps(name, shape):
            return ctx.enter_context(nc.psum_tensor(name, shape, F32))

        def sem(name):
            return ctx.enter_context(nc.semaphore(name))

        slot = [sb(f"slot{j}", [P, ROWS, WW]) for j in range(KH)]
        slotf = [s[:, :, :].rearrange("p h w -> p (h w)") for s in slot]
        u_col = sb("u_col", [P, WW, HH])
        ucf = u_col[:, :, :].rearrange("p w h -> p (w h)")
        hs = sb("hs", [P, L])
        head = hs[:, HEAD:HEAD + (CR + 1) * WW].rearrange("p (h w) -> p h w", w=WW)
        tab = sb("tab", [P, 2, CH])
        state = sb("state", [P, 2])
        xa = [sb(f"xa{e}", [P, TILES, D]) for e in range(2)]
        xn_x = sb("xn_x", [P, TILES, D])
        xt_x = sb("xt_x", [P, KH, JOB])
        xs = sb("xs", [P, KH, JOB])
        bst = sb("bst", [P, TILES, 6])
        pre = sb("pre", [P, CR, WW])
        xg = [sb(f"xg{e}", [P, TILES, D]) for e in range(2)]
        xn_g = sb("xn_g", [P, TILES, D])
        xo = sb("xo", [P, TILES, D])
        xt_g = sb("xt_g", [P, KH, JOB])
        y = sb("y", [P, KH, JOB])
        sg = sb("sg", [P, KH, JOB])
        ln_all = sb("ln_all", [P, JOBS, 2 * TILES])
        ln_x = sb("ln_x", [P, 2 * TILES])
        ln_gt = sb("ln_gt", [P, 2 * TILES])
        lt = sb("lt", [P, 4, TILES])
        mhalf = sb("mhalf", [P, TILES])
        w_in_sb = sb("w_in_sb", [P, KH, 2 * D])
        w_out_sb = sb("w_out_sb", [P, KH, D])
        ident = sb("ident", [P, P])
        more_first = sg[:, :, :].rearrange("p k t -> p (k t)")[:, 0:2 * KH * P].rearrange(
            "p (t j c) -> p t j c", t=2, j=KH)
        more_last = xt_x[:, :, :].rearrange("p k t -> p (k t)")[:, 0:KH * P].rearrange(
            "p (t j c) -> p t j c", t=1, j=KH)
        diag = sb("diag", [P, NT, KH, P])
        cw = sb("cw", [P, 9, KH])
        cols = sb("cols", [P, 10, KH])
        g_c, b_c, bx_c, bg_c, cb_c, al_c, sb_c, sc_c, sd_c, kap = [cols[:, i, :] for i in range(10)]
        more = sb("more", [P, 6, KH])
        a_c, la_c, nla_c, del_c, hbg_c, tmp_c = [more[:, i, :] for i in range(6)]
        bo, bo_rest, bo_sum = [xn_g[:, i, :] for i in range(TILES)]
        bo3 = sb("bo3", [P, D], BF16)
        ones3 = sb("ones3", [P, P], BF16)

        ps_x = ps("ps_x", [P, 2, 512])
        ps_g = ps("ps_g", [P, 2, 512])
        ps_c = ps("ps_c", [P, 2, 512])
        ps_o = ps("ps_o", [P, 2, 512])
        ps_of = ps_o[:, :, :].rearrange("p a b -> p (a b)")

        set_in = sem("set_in")
        set_steps = sem("set_steps")
        tab_arg = sem("tab_arg")
        tab_exp = sem("tab_exp")
        set_v = sem("set_v")
        set_a = sem("set_a")
        set_done = sem("set_done")
        more_made = sem("more_made")
        tab_made = sem("tab_made")
        passed = sem("passed")
        tab_stored = sem("tab_stored")
        x_loaded = [sem(f"x_loaded{e}") for e in range(2)]
        x_stats = sem("x_stats")
        x_nums = sem("x_nums")
        x_norm = sem("x_norm")
        x_turned = sem("x_turned")
        x_evac = sem("x_evac")
        x_proj = sem("x_proj")
        x_out = sem("x_out")
        xin_stored = sem("xin_stored")
        ln_step = sem("ln_step")
        ln_copied = sem("ln_copied")
        xin_loaded = [sem(f"xin_loaded{r}") for r in range(PIECES)]
        head_loaded = sem("head_loaded")
        conv_summed = sem("conv_summed")
        conv_taken = sem("conv_taken")
        conv_tap = sem("conv_tap")
        silu_done = sem("silu_done")
        conv_out = sem("conv_out")
        tab_loaded = [sem(f"tab_loaded{k}") for k in range(2)]
        scan_f = sem("scan_f")
        scan_b = sem("scan_b")
        ucol_ready = sem("ucol_ready")
        state_saved = sem("state_saved")
        d_added = sem("d_added")
        rows_added = sem("rows_added")
        cols_added = sem("cols_added")
        s_ready = sem("s_ready")
        s_stored = [sem(f"s_stored{r}") for r in range(PIECES)]
        xg_loaded = [sem(f"xg_loaded{e}") for e in range(2)]
        sg_loaded = sem("sg_loaded")
        g_norm = sem("g_norm")
        g_turned = sem("g_turned")
        g_evac = sem("g_evac")
        g_proj = sem("g_proj")
        g_act = sem("g_act")
        y_done = sem("y_done")
        o_proj = sem("o_proj")
        o_added = sem("o_added")
        o_stored = sem("o_stored")

        N_IN = 15

        def base(eng, *sems, by=1):
            for s in sems:
                eng.sem_inc(s, by)

        def wait_alone(eng, s, value):
            eng.wait_ge(s, value)
            eng.sem_inc(passed, 1)

        def x_job(n, s):
            return (n + 3) * PER_UNIT + s

        def g_job(n, s):
            return (n - 2) * PER_UNIT + s

        def pair_of(job_of, n, s, e):
            return (job_of(n, 0) // 2 if isinstance(n, int) else
                    (n + (3 if job_of is x_job else -2)) * HALF) + (s - e) // 2

        def stores_up_to(i):
            return 2 * i + 2 * -(-i // PARTS)

        def turned_x(gate):
            return ps_x if gate else ps_g

        def set_up_step(n, s):
            return (n + 3) * PER_UNIT + s if isinstance(n, int) and isinstance(s, int) and n < -1 else -1

        def taps_moved(n):
            return (0 if not isinstance(n, int) else 2 if n in (0, 1) else 1 if n in (UNITS - 3, UNITS - 2) else 0)

        def tap_done(g, t):
            return g * (ND - 1) + t + 1

        def xin_image(n, par):
            return (n - par) // 2 + par

        def x_image(n, par):
            return (n - par) // 2 + 1 + par

        def g_image(n, par):
            return (n - par) // 2 - 1

        def s_image(n, par):
            return (n - par) // 2 - 1 + par

        def store_conv_input(eng, n, par, s):
            wait_alone(eng, x_out, finished(x_job(n, s)))
            eng.dma_start(xin_d[x_image(n, par)][:, :, bass.ds((s + (1 - par) * PER_UNIT) * JOB, JOB)]
                          .rearrange("k p t -> p k t"), xs[:, :, :]).then_inc(xin_stored, 16)

        block = ctx.enter_context(nc.Block())

        @block.sync
        def _(sp):
            def col(v, width=KH):
                return v.rearrange("(j p) -> p j", p=P)

            base(sp, xin_stored, o_stored, by=16)

            def load_x(g, e):
                sp.dma_start(xa[e][:, :, :], x_t[bass.ds(g, 1)].rearrange("o p i d -> (o p) i d")
                             ).then_inc(x_loaded[e], 16)

            def load_xg(g, e):
                sp.dma_start(xg[e][:, :, :], x_t[bass.ds(g, 1)].rearrange("o p i d -> (o p) i d")
                             ).then_inc(xg_loaded[e], 16)

            for g in range(2):
                load_x(g, g)
            with nc.allow_non_contiguous_dma(reason="small per-channel vectors, once"):
                sp.dma_start(w_in_sb[:, :, :], w_in.rearrange("(k p) n -> p k n", p=P)).then_inc(set_in, 16)
                sp.dma_start(w_out_sb[:, :, :], w_out.rearrange("(k p) n -> p k n", p=P)).then_inc(set_in, 16)
                sp.dma_start(ident[:, :], ident_in).then_inc(set_in, 16)
                for dst, src in ((g_c, col(ln_g)), (b_c, col(ln_b)), (cb_c, col(conv_b)), (al_c, col(a_logit)),
                                 (sb_c, col(ssm_b)), (sc_c, col(ssm_c)), (sd_c, col(ssm_d)),
                                 (bx_c, col(b_in[0:D])), (bg_c, col(b_in[D:2 * D]))):
                    sp.dma_start(dst, src).then_inc(set_in, 16)
                cwv = conv_w.rearrange("a b o (j p) -> p (a b o) j", p=P)
                for j in range(KH):
                    sp.dma_start(cw[:, :, j], cwv[:, :, j]).then_inc(set_in, 16)
                sp.dma_start(bo, b_out.rearrange("(o d) -> o d", o=1).broadcast_to([P, D])).then_inc(set_in, 16)
                sp.dma_start(ucf[:, 0:TP], steps_in.broadcast_to([P, TP])).then_inc(set_steps, 16)

            def store_ratios(i):
                j, part = i // PARTS, i % PARTS
                lo, hi = part * TP, (part + 1) * TP
                sp.wait_ge(tab_made, i + 1)
                if i:
                    sp.wait_ge(tab_stored, 16 * stores_up_to(i))
                for h in range(2):
                    sp.dma_start(tab_d[h, j, :, lo:hi], hs[:, lo:hi]).then_inc(tab_stored, 16)
                    if part == 0:
                        k = j if h == 0 else 1 - j
                        sp.dma_start(tab_d[h, k, :, L:L + TP], hs[:, 0:TP]).then_inc(tab_stored, 16)

            def period(n, par, x=False, conv=False, scan=False, gate=False):
                static = isinstance(n, int)
                final_x = static and x and n == UNITS - 4
                final_g = static and gate and n == UNITS + 1

                def store_sums(r):
                    if r == 0:
                        wait_alone(sp, s_ready, n)
                    lo, hi = WW * SUM_ROWS[r], WW * SUM_ROWS[r + 1]
                    sp.dma_start(s_d[s_image(n, par), 1 - par, :, lo:hi], slotf[1 - par][:, lo:hi]
                                 ).then_inc(s_stored[r], 16)

                def load_conv_input(r):
                    jobs = (xin_image(n, par) + 1) * (L // JOB)
                    if r == 0:
                        wait_alone(sp, xin_stored, (jobs - L // JOB // 2) * 16 + 16)
                    elif IN_ROWS[r + 1] > HH // 2 >= IN_ROWS[r]:
                        wait_alone(sp, xin_stored, jobs * 16 + 16)
                    if not static or n >= 1:
                        wait_alone(sp, s_stored[r], n * 16)
                    sp.dma_start(slot[1 - par][:, 2 + IN_ROWS[r]:2 + IN_ROWS[r + 1], :].rearrange("p h w -> p (h w)"),
                                 xin_d[xin_image(n, par), 1 - par, :, WW * IN_ROWS[r]:WW * IN_ROWS[r + 1]]
                                 ).then_inc(xin_loaded[r], 16)

                def load_head():
                    image = (n - par) // 2 + 1
                    wait_alone(sp, xin_stored, (image * (L // JOB) + L // JOB // 2) * 16 + 16)
                    if scan:
                        wait_alone(sp, cols_added, n * (2 * PER_UNIT) + PER_UNIT)
                    sp.dma_start(hs[:, HEAD:HEAD + (CR + 1) * WW], xin_d[image, par, :, 0:(CR + 1) * WW]
                                 ).then_inc(head_loaded, 16)

                tail = gate and not scan
                storing = (scan or gate) and (not static or 1 <= n <= UNITS)

                def step(s, e):
                    fixed = isinstance(s, int)
                    half = s // HALF if fixed else 1
                    if x and not (final_x and s >= PER_UNIT - 2):
                        g = x_job(n, s) + 2
                        wait_alone(sp, x_norm, g)
                        load_x(g, e)
                    if 2 <= set_up_step(n, s) < 2 * PARTS + 2:
                        store_ratios(set_up_step(n, s) - 2)
                    if storing and fixed and s == 0:
                        store_sums(0)
                    if storing and fixed and s == 0:
                        store_sums(1)
                    if gate:
                        g = g_job(n, s)
                        if fixed and par == 0 and s in (0, HALF // 2):
                            wait_alone(sp, s_stored[s // (HALF // 2)], n * 16)
                        wait_alone(sp, y_done, before(g))
                        sp.dma_start(sg[:, :, :],
                                     s_d[g_image(n, par)][:, :, bass.ds((s + par * PER_UNIT) * JOB, JOB)]
                                     .rearrange("k p t -> p k t")).then_inc(sg_loaded, 16)
                    if conv and fixed and s == 0:
                        load_conv_input(0)
                    if gate and not (final_g and s == PER_UNIT - 1):
                        g = g_job(n, s) + 1
                        if tail:
                            wait_alone(sp, g_norm, g)
                            if n == UNITS and isinstance(s, int) and s < 2:
                                wait_alone(sp, o_added, g)
                        else:
                            wait_alone(sp, o_added, g)
                        load_xg(g, 1 - e)
                    if scan:
                        for k in range(2):
                            pr = n * (2 * PER_UNIT) + (s * 2 + (2 + k))
                            wait_alone(sp, scan_b, pr + 1)
                            sp.dma_start(tab[:, k, :],
                                         tab_d[half, par, :, bass.ds((s * 2 + (2 + k - PER_UNIT * half)) * CH, CH)]
                                         ).then_inc(tab_loaded[k], 16)
                    if conv and fixed and s < PIECES - 1:
                        load_conv_input(s + 1)
                    if storing and fixed and s < PIECES - 2:
                        store_sums(s + 2)
                    if x and gate:
                        store_conv_input(sp, n, par, s)
                    if tail:
                        g = g_job(n, s)
                        wait_alone(sp, o_added, g)
                        sp.dma_start(xa[e][:, :, :], x_t[bass.ds(g, 1)].rearrange("o p i d -> (o p) i d")
                                     ).then_inc(x_loaded[e], 16)

                if static and n == UNITS:
                    sp.wait_ge(x_norm, JOBS + 1)
                if gate and static and n == 2:
                    sp.wait_ge(conv_summed, finished(3 * PER_UNIT - 1))
                    load_xg(0, 0)
                run_steps(sp, 0, True, step)
                if gate and par == 0:
                    for r in range(2, SUM_ROWS.index(HH // 2) if conv else PIECES):
                        wait_alone(sp, s_stored[r], n * 16)
                run_steps(sp, 1, final_x or final_g or (static and n == -3), step)
                if static and n == -2:
                    sp.wait_ge(tab_stored, 16 * stores_up_to(2 * PARTS))
                    for k in range(2):
                        sp.dma_start(tab[:, k, :], tab_d[0, 0, :, k * CH:(k + 1) * CH]).then_inc(tab_loaded[k], 16)
                if not static or -2 <= n <= UNITS - 3:
                    load_head()

            run_periods(sp, period, IMAGES)
            for r in range(PIECES):
                sp.wait_ge(s_stored[r], 16 * UNITS)
            for k in range(2):
                sp.wait_ge(tab_loaded[k], 16 * (UNITS * PER_UNIT + 1))
            sp.wait_ge(xin_stored, 16 * (JOBS + 1))
            sp.wait_ge(o_stored, 16 * (JOBS + 1))

        @block.tensor
        def _(pe):
            base(pe, x_turned, x_proj, g_turned, g_proj, o_proj, conv_summed)
            pe.wait_ge(set_in, 16 * N_IN)

            def turn(ps_t, src, done):
                for t in range(TILES):
                    for k in range(KH):
                        ins = pe.transpose(ps_t[:, k, t * P:(t + 1) * P], src[:, t, k * P:(k + 1) * P], ident[:, :])
                ins.then_inc(done, 1)

            def project(ps_t, src, first, done):
                for j in range(KH):
                    for k in range(KH):
                        ins = pe.matmul(ps_t[:, j, 0:JOB], w_in_sb[:, k, first + j * P:first + (j + 1) * P],
                                        src[:, k, :], start=(k == 0), stop=(k == KH - 1))
                ins.then_inc(done, 1)

            def conv_taps(j, s, g, parts, moved):
                if 0 in parts:
                    pe.wait_ge(conv_taken, before(g))
                hr = CR // 2
                for r in parts:
                    acc = ps_c[:, r, 0:JOB].rearrange("p (h w) -> p h w", w=WW)
                    taps = [(d, diag[:, t, j, :]) for t, d in enumerate(PE_TAPS)]
                    for t in range(moved):
                        taps.append((DVE_TAPS[ND - 1 - t], (more_first if moved == 2 else more_last)[:, t, j, :]))
                    for t, ((dh, dw), weights) in enumerate(taps):
                        lo, hi = max(0, -dw), WW - max(0, dw)
                        first = isinstance(s, int) and s == 0
                        top = 1 if first and r == 0 and dh < 0 else 0
                        row = hr * r + dh + top
                        src = head[:, row:row + hr - top] if first else \
                            slot[j][:, bass.ds(s * CR + (row + 2), hr - top), :]
                        ins = pe.matmul(acc[:, top:hr, lo:hi], weights, src[:, :, lo + dw:hi + dw],
                                        start=(t == 0), stop=(t == len(taps) - 1))
                if 1 in parts:
                    ins.then_inc(conv_summed, 1)

            def wait_piece(n, s):
                if isinstance(s, int):
                    for r in range(PIECES):
                        if s == FIRST_CHUNK[r]:
                            pe.wait_ge(xin_loaded[r], (n + 1) * 16 + 16)
                    if s == 0:
                        pe.wait_ge(head_loaded, (n + 1) * 16 + 16)

            def project_out(g):
                pe.wait_ge(y_done, finished(g))
                pe.wait_ge(o_added, before(g))
                for t in range(TILES):
                    o = ps_of[:, t * D:(t + 1) * D]
                    pe.matmul(o, ones3[:, :], bo3[:, :], start=True, stop=False)
                    for k in range(KH):
                        ins = pe.matmul(o, y[:, k, t * P:(t + 1) * P], w_out_sb[:, k, :],
                                        start=False, stop=(k == KH - 1))
                ins.then_inc(o_proj, 1)

            def period(n, par, x=False, conv=False, scan=False, gate=False):
                static = isinstance(n, int)
                if static and n == -1:
                    pe.wait_ge(set_done, 1)
                if static and n == UNITS - 3:
                    pe.wait_ge(more_made, 1)

                def step(s, e):
                    gx, gg, gc = x_job(n, s), g_job(n, s), (n + 1) * PER_UNIT + s
                    if conv and not scan:
                        wait_piece(n, s)
                        conv_taps(1 - par, s, gc, (0,), taps_moved(n))
                    if gate:
                        pe.wait_ge(g_norm, finished(gg))
                        pe.wait_ge(g_act, before(gg))
                        turn(ps_g, xn_g, g_turned)
                    if x:
                        pe.wait_ge(x_norm, finished(gx))
                        if gate:
                            pe.wait_ge(x_out, before(gx))
                        else:
                            pe.wait_ge(x_evac, before(gx))
                        turn(turned_x(gate), xn_x, x_turned)
                    if gate and not scan and not (n == UNITS and isinstance(s, int) and s == 0):
                        project_out(gg - 1)
                    if conv:
                        if scan:
                            wait_piece(n, s)
                        conv_taps(1 - par, s, gc, (0,) if scan else (1,), taps_moved(n))
                    if gate:
                        pe.wait_ge(g_evac, finished(gg))
                        project(ps_g, xt_g, D, g_proj)
                    if conv and scan:
                        conv_taps(1 - par, s, gc, (1,), taps_moved(n))
                    if x:
                        pe.wait_ge(x_evac, finished(gx))
                        pe.wait_ge(x_out, before(gx))
                        project(ps_x, xt_x, 0, x_proj)
                    if gate and scan:
                        project_out(gg)

                run_steps(pe, 0, True, step)
                if conv:
                    wait_alone(pe, xin_loaded[PIECES - 1], (n + 1) * 16 + 16)
                run_steps(pe, 1, False, step)
                if static and n == UNITS + 1:
                    project_out(JOBS - 1)

            run_periods(pe, period, IMAGES)

        @block.scalar
        def _(act):
            base(act, x_norm, g_norm, x_evac, x_out, g_evac, g_act, conv_out, silu_done)
            act.wait_ge(set_in, 16 * N_IN)
            act.activation(tmp_c, al_c, ACT.Exp, scale=-1.0).then_inc(set_a, 1)
            act.wait_ge(set_v, 3)
            act.activation(la_c, a_c, ACT.Ln).then_inc(set_a, 1)

            def norm(dst, src, numbers, done):
                for t in range(TILES):
                    ins = act.activation(dst[:, t, :], src[:, t, :], ACT.Identity,
                                         bias=numbers[:, TILES + t:TILES + t + 1], scale=numbers[:, t:t + 1])
                ins.then_inc(done, 1)

            def norm_x(g, e):
                wait_alone(act, x_nums, finished(g))
                wait_alone(act, x_turned, before(g))
                norm(xn_x, xa[e], ln_x, x_norm)

            def norm_g(g, e, pair):
                wait_alone(act, ln_copied, g + 1)
                wait_alone(act, xg_loaded[e], pair * 16 + 16)
                wait_alone(act, g_turned, before(g))
                norm(xn_g, xg[e], ln_gt, g_norm)

            def silu(j, s, g):
                act.wait_ge(conv_tap, tap_done(g, ND - 1))
                act.activation(pre[:, :, :], pre[:, :, :], ACT.Silu, bias=cb_c[:, j:j + 1]).then_inc(silu_done, 1)
                act.wait_ge(silu_done, finished(g))
                act.activation(slot[j][:, bass.ds(s * CR, CR), :], pre[:, :, :], ACT.Copy,
                               scale=kap[:, j:j + 1]).then_inc(conv_out, 1)

            def store_out(g):
                wait_alone(act, o_added, finished(g))
                act.dma_start(out_t[bass.ds(g, 1)].rearrange("o p i d -> (o p) i d"), xo[:, :, :]
                              ).then_inc(o_stored, 16)

            def period(n, par, x=False, conv=False, scan=False, gate=False):
                static = isinstance(n, int)
                final_x = static and x and n == UNITS - 4
                final_g = static and gate and n == UNITS + 1
                if static and n == -1:
                    act.wait_ge(set_done, 1)
                if gate and static and n == 2:
                    norm_g(0, 0, 0)

                def step(s, e):
                    fixed = isinstance(s, int)
                    gx, gg, gc = x_job(n, s), g_job(n, s), (n + 1) * PER_UNIT + s
                    if gate:
                        act.wait_ge(g_turned, finished(gg))
                        act.wait_ge(g_proj, before(gg))
                        for k in range(KH):
                            ins = act.activation(xt_g[:, k, :], ps_g[:, k, 0:JOB], ACT.Identity,
                                                 bias=b_c[:, k:k + 1], scale=g_c[:, k:k + 1])
                        ins.then_inc(g_evac, 1)
                    if gate and not scan and not (final_g and s == PER_UNIT - 1):
                        norm_g(gg + 1, 1 - e, pair_of(g_job, n, s, e) + e)
                    if x:
                        act.wait_ge(x_turned, finished(gx))
                        act.wait_ge(x_proj, before(gx))
                        for k in range(KH):
                            ins = act.activation(xt_x[:, k, :], turned_x(gate)[:, k, 0:JOB], ACT.Identity,
                                                 bias=b_c[:, k:k + 1], scale=g_c[:, k:k + 1])
                        ins.then_inc(x_evac, 1)
                    if static and n < 2 or static and n == 2 and fixed and s == 0:
                        if not fixed or s > 0:
                            store_conv_input(act, n, par, s - 1)
                        elif n > -3:
                            store_conv_input(act, n - 1, 1 - par, PER_UNIT - 1)
                    if scan and fixed and s == 0:
                        silu(par, PER_UNIT - 1, gc - 1)
                    if gate and not (static and n == 2 and fixed and s == 0):
                        store_out(gg - 1)
                    if conv and fixed and s == 1:
                        act.wait_ge(xin_loaded[0], (n + 1) * 16 + 16)
                    if conv and not (fixed and s == 0):
                        silu(1 - par, s - 1, gc - 1)
                    if scan and fixed and s < STEPS:
                        if s == 0:
                            act.wait_ge(conv_out, finished(n * PER_UNIT + (PER_UNIT - 1)))
                            if not static or n >= 1:
                                act.wait_ge(s_ready, n)
                        R = HH // STEPS
                        act.activation(u_col[:, :, R * s:R * (s + 1)].rearrange("p w h -> p h w"),
                                       slot[par][:, R * s:R * (s + 1), :], ACT.Copy).then_inc(ucol_ready, 1)
                    if gate:
                        act.wait_ge(g_proj, finished(gg))
                        act.wait_ge(o_proj, before(gg))
                        for j in range(KH):
                            ins = act.activation(y[:, j, :], ps_g[:, j, 0:JOB], ACT.Tanh,
                                                 bias=hbg_c[:, j:j + 1], scale=0.5)
                        ins.then_inc(g_act, 1)
                    if x and not (final_x and s == PER_UNIT - 1):
                        norm_x(gx + 1, 1 - e)
                    late = fixed and s == 0
                    if scan and gate and not late:
                        norm_g(gg + 1, 1 - e, pair_of(g_job, n, s, e) + e)
                    if x:
                        act.wait_ge(x_proj, finished(gx))
                        act.wait_ge(xin_stored, gx * 16 + 16)
                        for j in range(KH):
                            ins = act.activation(xs[:, j, :], ps_x[:, j, 0:JOB], ACT.Identity,
                                                 bias=bx_c[:, j:j + 1])
                        ins.then_inc(x_out, 1)
                    if scan and gate and late:
                        norm_g(gg + 1, 1 - e, pair_of(g_job, n, s, e) + e)
                    if 0 <= set_up_step(n, s) < 2 * PARTS:
                        i = set_up_step(n, s)
                        part = hs[:, (i % PARTS) * TP:(i % PARTS + 1) * TP]
                        act.wait_ge(tab_arg, 2 * i + 2)
                        act.activation(part, part, ACT.Exp).then_inc(tab_exp, 1)

                run_steps(act, 0, True, step)
                run_steps(act, 1, final_x or final_g or (static and n == -3), step)

            norm_x(0, 0)
            run_periods(act, period, IMAGES)
            store_out(JOBS - 1)

        @block.gpsimd
        def _(pool):
            base(pool, x_nums, ln_step)
            pool.memset(mhalf[:, :], -0.5).then_inc(ln_step, 1)
            LN_OPS = 10

            def period(n, par, x=False, conv=False, scan=False, gate=False):
                def step(s, e):
                    if x:
                        g = x_job(n, s)
                        c = g * LN_OPS + 2
                        pool.wait_ge(x_stats, finished(g))
                        pool.wait_ge(ln_step, c)
                        pool.wait_ge(x_nums, before(g))
                        pool.tensor_tensor(lt[:, 0, :], bst[:, :, 1], bst[:, :, 4], ALU.add).then_inc(ln_step, 1)
                        pool.tensor_tensor(lt[:, 1, :], bst[:, :, 1], bst[:, :, 4], ALU.subtract).then_inc(ln_step, 1)
                        pool.tensor_tensor(lt[:, 2, :], bst[:, :, 2], bst[:, :, 5], ALU.add).then_inc(ln_step, 1)
                        pool.wait_ge(ln_step, c + 3)
                        pool.tensor_tensor(lt[:, 1, :], lt[:, 1, :], lt[:, 1, :], ALU.mult).then_inc(ln_step, 1)
                        wait_alone(pool, ln_step, c + 4)
                        pool.tensor_scalar(lt[:, 1, :], lt[:, 1, :], D / 4.0, 0.0, ALU.mult, ALU.add).then_inc(ln_step, 1)
                        pool.wait_ge(ln_step, c + 5)
                        pool.tensor_tensor(lt[:, 2, :], lt[:, 1, :], lt[:, 2, :], ALU.add).then_inc(ln_step, 1)
                        wait_alone(pool, ln_step, c + 6)
                        pool.tensor_scalar(lt[:, 2, :], lt[:, 2, :], 1.0 / D, LN_EPS, ALU.mult, ALU.add).then_inc(ln_step, 1)
                        pool.wait_ge(ln_step, c + 7)
                        pool.wait_ge(x_norm, before(g))
                        pool.tensor_tensor(ln_x[:, 0:TILES], lt[:, 2, :], mhalf[:, :], ALU.pow).then_inc(ln_step, 1)
                        pool.tensor_scalar(lt[:, 0, :], lt[:, 0, :], -0.5, 0.0, ALU.mult, ALU.add).then_inc(ln_step, 1)
                        pool.wait_ge(ln_step, c + 9)
                        pool.tensor_tensor(ln_x[:, TILES:2 * TILES], lt[:, 0, :], ln_x[:, 0:TILES], ALU.mult).then_inc(ln_step, 1)
                        pool.wait_ge(ln_step, c + 10)
                        pool.tensor_copy(ln_all[:, bass.ds(g, 1), :].rearrange("p o t -> p (o t)"), ln_x[:, :]
                                         ).then_inc(x_nums, 1)
                    if gate:
                        g = g_job(n, s)
                        pool.wait_ge(g_norm, before(g))
                        pool.tensor_copy(ln_gt[:, :], ln_all[:, bass.ds(g, 1), :].rearrange("p o t -> p (o t)")
                                         ).then_inc(ln_copied, 1)

                for half in range(2):
                    run_steps(pool, half, False, step)

            run_periods(pool, period, IMAGES)

        @block.vector
        def _(dve):
            base(dve, x_stats, conv_taken, conv_tap, scan_f, y_done, o_added)
            base(dve, scan_b, by=2)
            for j in range(KH):
                dve.memset(slot[j][:, ROWS - 1, :], 0.0)
            dve.memset(ones3[:, :], 1.0)

            dve.wait_ge(set_a, 1)
            dve.tensor_scalar(tmp_c, tmp_c, 1.0, None, ALU.add).then_inc(set_v, 1)
            dve.wait_ge(set_v, 1)
            dve.reciprocal(tmp_c, tmp_c).then_inc(set_v, 1)
            dve.wait_ge(set_v, 2)
            dve.tensor_scalar(a_c, tmp_c, A_EPS, 1.0 - A_EPS, ALU.max, ALU.min).then_inc(set_v, 1)
            dve.wait_ge(set_a, 2)
            dve.tensor_scalar(nla_c, la_c, -1.0, None, ALU.mult).then_inc(set_v, 1)
            dve.wait_ge(set_v, 4)

            def ratios(i):
                j, lo = i // PARTS, (i % PARTS) * TP
                part = hs[:, lo:lo + TP]
                if i == 0:
                    dve.wait_ge(set_steps, 16)
                if j:
                    dve.wait_ge(tab_stored, 16 * stores_up_to(i - PARTS + 1))
                dve.tensor_scalar(part, ucf[:, 0:TP], float(lo), nla_c[:, j:j + 1], ALU.add, ALU.mult).then_inc(tab_arg, 1)
                dve.wait_ge(tab_arg, 2 * i + 1)
                dve.tensor_scalar(part, part, LOG_MIN, 0.0, ALU.add, ALU.min).then_inc(tab_arg, 1)

            def clamp_ratios(i):
                j, lo = i // PARTS, (i % PARTS) * TP
                part = hs[:, lo:lo + TP]
                dve.wait_ge(tab_exp, i + 1)
                dve.tensor_scalar(part, part, 1.0, a_c[:, j:j + 1], ALU.min, ALU.max).then_inc(tab_made, 1)

            def make_scales():
                dve.wait_ge(set_in, 16 * N_IN)
                dve.tensor_tensor(tmp_c, sb_c, sc_c, ALU.mult).then_inc(set_v, 1)
                dve.wait_ge(set_v, 5)
                dve.tensor_scalar(kap, tmp_c, 0.125, None, ALU.mult).then_inc(set_v, 1)
                dve.wait_ge(set_v, 6)
                dve.tensor_tensor(tmp_c, kap, kap, ALU.mult).then_inc(set_v, 1)
                dve.wait_ge(set_v, 7)
                dve.tensor_scalar(tmp_c, tmp_c, TINY * TINY, 2.0 * TINY, ALU.is_lt, ALU.mult).then_inc(set_v, 1)
                dve.wait_ge(set_v, 8)
                dve.tensor_tensor(kap, kap, tmp_c, ALU.add).then_inc(set_v, 1)
                dve.wait_ge(set_v, 9)
                dve.reciprocal(tmp_c, kap).then_inc(set_v, 1)
                dve.wait_ge(set_v, 10)
                dve.scalar_tensor_tensor(out=del_c, in0=sd_c, scalar=0.5, in1=tmp_c, op0=ALU.mult, op1=ALU.mult
                                         ).then_inc(set_v, 1)
                dve.tensor_scalar(hbg_c, bg_c, 0.5, None, ALU.mult).then_inc(set_v, 1)

            def make_diagonal(where, t):
                dh, dw = DVE_TAPS[ND - 1 - t]
                tap = (dh + 1) * 3 + dw + 1
                for j in range(KH):
                    ins = dve.tensor_scalar(where[:, t, j, :], ident[:, :], cw[:, tap, j:j + 1], None, ALU.mult)
                return ins

            def make_diagonals():
                for t, (dh, dw) in enumerate(PE_TAPS):
                    tap = (dh + 1) * 3 + dw + 1
                    for j in range(KH):
                        dve.tensor_scalar(diag[:, t, j, :], ident[:, :], cw[:, tap, j:j + 1], None, ALU.mult)

                for t in range(2):
                    make_diagonal(more_first, t)

            def make_bias_rows():
                dve.tensor_copy(bo3[:, :], bo).then_inc(set_v, 1)
                dve.wait_ge(set_v, 13)
                dve.tensor_scalar(bo_sum, bo3[:, :], ident[:, 0:1], None, ALU.mult).then_inc(set_v, 1)
                dve.tensor_tensor(bo_rest, bo, bo3[:, :], ALU.subtract).then_inc(set_v, 1)
                for r in range(1, 3):
                    dve.wait_ge(set_v, 15 + 3 * (r - 1))
                    dve.tensor_copy(bo3[:, :], bo_rest).then_inc(set_v, 1)
                    dve.wait_ge(set_v, 16 + 3 * (r - 1))
                    dve.scalar_tensor_tensor(out=bo_sum, in0=bo3[:, :], scalar=ident[:, r:r + 1], in1=bo_sum,
                                             op0=ALU.mult, op1=ALU.add).then_inc(set_v, 1)
                    dve.tensor_tensor(bo_rest, bo_rest, bo3[:, :], ALU.subtract).then_inc(set_v, 1)
                dve.wait_ge(set_v, 21)
                dve.tensor_copy(bo3[:, :], bo_sum).then_inc(set_v, 1)
                dve.wait_ge(set_v, 22)
                dve.memset(state[:, :], 0.0).then_inc(set_done, 1)

            def stats(g, e, pair):
                dve.wait_ge(x_loaded[e], pair * 16 + 16)
                dve.wait_ge(x_nums, before(g))
                for t in range(TILES):
                    ins = dve.bn_stats(bst[:, t, :], xa[e][:, t, :])
                ins.then_inc(x_stats, 1)

            def tap(j, s, g, t, moved):
                dh, dw = DVE_TAPS[t]
                w = cw[:, (dh + 1) * 3 + dw + 1, j:j + 1]
                top = 1 if isinstance(s, int) and s == 0 and dh < 0 else 0
                src = head[:, dh + top:dh + CR] if isinstance(s, int) and s == 0 else \
                    slot[j][:, bass.ds(s * CR + (2 + dh + top), CR - top), :]
                if t == 0:
                    dve.wait_ge(conv_summed, finished(g))
                    dve.wait_ge(conv_out, before(g))
                    dve.scalar_tensor_tensor(
                        out=pre[:, :, :].rearrange("p (a h) w -> p a (h w)", a=2),
                        in0=src.rearrange("p (a h) w -> p a (h w)", a=2), scalar=w,
                        in1=ps_c[:, :, 0:JOB], op0=ALU.mult, op1=ALU.add).then_inc(conv_taken, 1)
                    return
                lo, hi = max(0, -dw), WW - max(0, dw)
                if t == 1:
                    dve.wait_ge(conv_taken, finished(g))
                else:
                    dve.wait_ge(conv_tap, tap_done(g, t - 1))
                dve.scalar_tensor_tensor(
                    out=pre[:, top:CR, lo:hi], in0=src[:, :, lo + dw:hi + dw], scalar=w,
                    in1=pre[:, top:CR, lo:hi], op0=ALU.mult, op1=ALU.add
                ).then_inc(conv_tap, 1 + moved if t == ND - 1 - moved else 1)

            def forward(n, src, phase, c):
                pr = n * (2 * PER_UNIT) + (PER_UNIT * phase + c)
                lo = c * CH
                dve.wait_ge(tab_loaded[c % 2], (n * PER_UNIT + (HALF * phase + c // 2)) * 16 + 16)
                dve.wait_ge(scan_f, before(pr))
                if c == 0:
                    init = 0.0
                elif c < HALF or (c == HALF and phase == 1):
                    init = hs[:, lo - 1:lo]
                elif c == HALF:
                    init = state[:, 0:1]
                else:
                    init = src[:, lo - 1:lo]
                dst = hs[:, lo:lo + CH] if c < HALF else src[:, lo:lo + CH]
                dve.tensor_tensor_scan(dst, tab[:, c % 2, :], src[:, lo:lo + CH], init, ALU.mult, ALU.add
                                       ).then_inc(scan_f, 1)

            def backward(n, src, phase, c):
                pr = n * (2 * PER_UNIT) + (PER_UNIT * phase + c)
                lo = L - (c + 1) * CH
                hi = lo + CH
                dve.wait_ge(scan_b, pr + 2)
                if c == 0:
                    init = 0.0
                elif c < HALF or (c == HALF and phase == 1):
                    init = hs[:, hi:hi + 1]
                elif c == HALF:
                    init = state[:, 1:2]
                else:
                    init = src[:, hi:hi + 1]
                flip = slice(hi - 1, lo - 1 if lo else None, -1)
                dst = hs[:, flip] if c < HALF else src[:, flip]
                dve.tensor_tensor_scan(dst, tab[:, c % 2, :], src[:, flip], init, ALU.mult, ALU.add
                                       ).then_inc(scan_b, 1)

            def add(n, par, q, c):
                u = slotf[par]
                lo = c * CH
                uv, hv = u[:, lo:lo + CH], hs[:, lo:lo + CH]
                if q == 0:
                    dve.scalar_tensor_tensor(out=hv, in0=uv, scalar=del_c[:, par:par + 1], in1=hv,
                                             op0=ALU.mult, op1=ALU.add).then_inc(d_added, 1)
                elif q == 1:
                    dve.tensor_tensor(uv, uv, hv, ALU.add).then_inc(rows_added, 1)
                else:
                    src = hs[:, lo:lo + CH].rearrange("p (w h) -> p h w", h=HH) if q == 2 else \
                        u_col[:, c * CR:(c + 1) * CR, :].rearrange("p w h -> p h w")
                    dst = slot[par][:, 0:HH, c * CR:(c + 1) * CR]
                    dve.tensor_tensor(dst, dst, src, ALU.add).then_inc(cols_added, 1)

            def settle_states(n):
                if not isinstance(n, int) or n >= 1:
                    dve.wait_ge(s_ready, n)
                pairs = n * (2 * PER_UNIT) + HALF
                dve.wait_ge(scan_f, pairs + 1)
                dve.wait_ge(scan_b, pairs + 2)
                dve.tensor_copy(state[:, 0:1], hs[:, L // 2 - 1:L // 2]).then_inc(state_saved, 1)
                dve.tensor_copy(state[:, 1:2], hs[:, L // 2:L // 2 + 1]).then_inc(state_saved, 1)

            def period(n, par, x=False, conv=False, scan=False, gate=False):
                static = isinstance(n, int)
                final_x = static and x and n == UNITS - 4
                final_g = static and gate and n == UNITS + 1
                if static and n == -1:
                    dve.wait_ge(set_done, 1)
                if static and n == UNITS - 3:
                    dve.wait_ge(x_proj, finished(JOBS - 1))
                    make_diagonal(more_last, 0).then_inc(more_made, 1)

                def add_residual(g, e, again=None):
                    tokens = xg[e] if again is None else xa[e]
                    dve.wait_ge(o_proj, finished(g))
                    dve.wait_ge(o_stored, g * 16 + 16)
                    if again is not None:
                        dve.wait_ge(x_loaded[e], (again + JOBS // 2) * 16 + 16)
                    dve.tensor_tensor(xo[:, :, :].rearrange("p t d -> p (t d)"), ps_of[:, 0:TILES * D],
                                      tokens[:, :, :].rearrange("p t d -> p (t d)"), ALU.add).then_inc(o_added, 1)

                def gate_values(g):
                    dve.wait_ge(g_act, finished(g))
                    dve.wait_ge(sg_loaded, g * 16 + 16)
                    dve.scalar_tensor_tensor(out=y[:, :, :], in0=y[:, :, :], scalar=1.0, in1=sg[:, :, :],
                                             op0=ALU.add, op1=ALU.mult).then_inc(y_done, 1)

                def pair_scans(s, k):
                    q = s // STEPS
                    phase, c = q // 2, HALF * (q % 2) + 2 * (s % STEPS) + k
                    src = slotf[par] if phase == 0 else ucf
                    if c == HALF and q == 1:
                        settle_states(n)
                        dve.wait_ge(state_saved, 2 * n + 2)
                        add(n, par, 0, c - 1)
                        add(n, par, 0, PER_UNIT - c)
                        dve.wait_ge(d_added, (n + 1) * PER_UNIT)
                        dve.wait_ge(ucol_ready, (n + 1) * STEPS)
                    if c == 0 and q == 2:
                        dve.wait_ge(scan_f, before(n * (2 * PER_UNIT) + PER_UNIT))
                        dve.wait_ge(scan_b, n * (2 * PER_UNIT) + (PER_UNIT + 2))
                        add(n, par, 1, PER_UNIT - 1)
                        add(n, par, 1, 0)
                        dve.wait_ge(rows_added, (n + 1) * PER_UNIT)
                    if conv and phase == 0 and c == HALF - 1:
                        dve.wait_ge(conv_summed, finished((n + 1) * PER_UNIT))
                        dve.wait_ge(conv_tap, tap_done((n + 1) * PER_UNIT, ND - 1))
                    forward(n, src, phase, c)
                    backward(n, src, phase, c)

                def pair_adds(s, k, scans=(0, 1)):
                    q = s // STEPS
                    phase, c = q // 2, HALF * (q % 2) + 2 * (s % STEPS) + k
                    if c == 0 or (c == HALF and q == 1):
                        return
                    qq = 2 if (q == 3 and c == HALF) else q
                    if q == 3 and c == HALF + 1:
                        dve.wait_ge(cols_added, n * (2 * PER_UNIT) + PER_UNIT)
                    pr = n * (2 * PER_UNIT) + (PER_UNIT * phase + c)
                    if 0 in scans:
                        dve.wait_ge(scan_f, finished(pr))
                        add(n, par, qq, c - 1)
                    if 1 in scans:
                        dve.wait_ge(scan_b, pr + 3)
                        add(n, par, qq, PER_UNIT - c)

                def step(s, e):
                    gx, gg, gc = x_job(n, s), g_job(n, s), (n + 1) * PER_UNIT + s
                    if gate and not scan and not (n == UNITS and s == 0):
                        tail_job = (n - UNITS) * PER_UNIT + s - 1
                        add_residual(gg - 1, 1 - e, tail_job // 2)
                    i = set_up_step(n, s)
                    if 0 <= i < 2 * PARTS:
                        ratios(i)
                    if 1 <= i <= 2 * PARTS:
                        clamp_ratios(i - 1)
                    if i == 2 * PARTS + 1:
                        make_scales()
                    if i == 2 * PARTS + 2:
                        make_diagonals()
                    if i == 2 * PARTS + 3:
                        make_bias_rows()
                    if scan:
                        if s == 0:
                            dve.wait_ge(conv_out, finished(n * PER_UNIT + (PER_UNIT - 1)))
                        pair_scans(s, 0)
                        pair_adds(s, 0)
                        pair_scans(s, 1)
                    if scan and s == 0:
                        pair_adds(s, 1)
                    if gate:
                        gate_values(gg)
                    for t in range(ND):
                        if conv and t < ND - taps_moved(n):
                            tap(1 - par, s, gc, t, taps_moved(n))
                        if scan and s > 0 and t < 2:
                            pair_adds(s, 1, (t,))
                        last = scan and s == PER_UNIT - 1
                        if t == 2 and x and not last and not (final_x and s >= PER_UNIT - 2):
                            stats(gx + 2, e, pair_of(x_job, n, s, e) + 1)
                        if t == 3 and gate and scan and not last:
                            add_residual(gg, e)

                straight = scan or conv or (static and (n < -1 or n >= UNITS))
                run_steps(dve, 0, straight, step)
                run_steps(dve, 1, straight, step)
                if final_g:
                    add_residual(JOBS - 1, 1, PER_UNIT - 1)
                if scan:
                    dve.wait_ge(scan_f, before(n * (2 * PER_UNIT) + 2 * PER_UNIT))
                    dve.wait_ge(scan_b, n * (2 * PER_UNIT) + (2 * PER_UNIT + 2))
                    add(n, par, 3, PER_UNIT - 1)
                    add(n, par, 3, 0)
                    dve.wait_ge(cols_added, (n + 1) * (2 * PER_UNIT))
                    dve.memset(state[:, :], 0.0).then_inc(s_ready, 1)
                    s = PER_UNIT - 1
                    if gate:
                        add_residual(g_job(n, s), 1)
                    if x and not final_x:
                        stats(x_job(n, s) + 2, 1, pair_of(x_job, n, s, 1) + 1)

            for g in range(2):
                stats(g, g, 0)
            run_periods(dve, period, IMAGES)


_INS = ["x", "ln_g", "ln_b", "w_in", "b_in", "conv_w", "conv_b", "a_logit", "ssm_b", "ssm_c", "ssm_d",
        "w_out", "b_out"]


def kernel(**inputs):
    import numpy as _np
    import concourse.bacc as _bacc
    from concourse import mybir as _mybir
    from concourse.bass_utils import run_bass_kernel_spmd as _run

    nc = _bacc.Bacc("TRN2", target_bir_lowering=False, num_devices=1)
    x = inputs["x"]
    tokens = x.shape[1] * x.shape[2]
    given = {n: inputs[n if n == "x" else "L0_conv_" + n] for n in _INS}
    given["ident"] = _np.eye(128, dtype=_np.float32)
    given["steps"] = _np.arange(-1, tokens // 6 - 1, dtype=_np.float32).reshape(1, -1)
    arrays, args = {}, []
    for name, a in given.items():
        a = _np.ascontiguousarray(a)
        arrays[f"in_{name}_dram"] = a
        args.append(nc.dram_tensor(f"in_{name}_dram", a.shape, _mybir.dt.from_np(a.dtype), kind="ExternalInput").ap())
    out = nc.dram_tensor("out_0_dram", x.shape, _mybir.dt.float32, kind="ExternalOutput").ap()
    conv_seq_kernel(nc, *args, out)
    r = _run(nc, [arrays], core_ids=[0])
    return r.results[0]["out_0_dram"]
```
